# Optimizing a Trainium2 kernel written in Bass

```python
import numpy as np
import jax
import jax.numpy as jnp

def _softmax(x, axis=-1):
    return jax.nn.softmax(x, axis=axis)

def _gelu(x):
    return jax.nn.gelu(x, approximate=True)

def _silu(x):
    return jax.nn.silu(x)

def _sigmoid(x):
    return jax.nn.sigmoid(x)

def _layernorm(x, axis=-1, eps=1e-05):
    m = jnp.mean(x, axis=axis, keepdims=True)
    v = jnp.var(x, axis=axis, keepdims=True)
    return (x - m) / jnp.sqrt(v + eps)

def _scatter_add(tgt, idx, src, axis=0):
    return tgt.at[idx].add(src)

def _segment_sum(src, seg, n):
    return jax.ops.segment_sum(src, seg, n)
kernel_name = 'mk_conv_seq_d4_conv_nchw128_r2_38d5db'

def setup_inputs(seed: int=0):
    np.random.seed(seed)
    _w = jnp.asarray

    def _rec_inputs():
        import jax
        import jax.numpy as jnp
        _gk = jax.random.key(seed)
        x = -0.0003957 + 1 * jax.random.normal(jax.random.fold_in(_gk, 1), (32, 64, 56, 56), jnp.float32)
        return x
    x = _rec_inputs()

    def _L0_conv_setup():
        import jax, jax.numpy as jnp
        import numpy as np
        from jax import lax
        EPS = 1e-05

        def _conv3x3(x, w):
            return lax.conv_general_dilated(x, w, window_strides=(1, 1), padding=((1, 1), (1, 1)), dimension_numbers=('NCHW', 'OIHW', 'NCHW'))

        def _batchnorm(y, gamma, beta):
            mean = jnp.mean(y, axis=(0, 2, 3), keepdims=True)
            var = jnp.var(y, axis=(0, 2, 3), keepdims=True)
            inv = lax.rsqrt(var + EPS)
            return (y - mean) * inv * gamma[None, :, None, None] + beta[None, :, None, None]
        key = jax.random.key(seed)
        k1, k2, k3 = jax.random.split(key, 3)
        N, C, H, W = (32, 64, 56, 56)
        x = jax.random.normal(k1, (N, C, H, W), dtype=jnp.float32)
        w1 = jax.random.normal(k2, (C, C, 3, 3), dtype=jnp.float32) * 0.05
        w2 = jax.random.normal(k3, (C, C, 3, 3), dtype=jnp.float32) * 0.05
        gamma1 = jnp.ones((C,), jnp.float32)
        beta1 = jnp.zeros((C,), jnp.float32)
        gamma2 = jnp.ones((C,), jnp.float32)
        beta2 = jnp.zeros((C,), jnp.float32)
        return {'x': x, 'w1': w1, 'gamma1': gamma1, 'beta1': beta1, 'w2': w2, 'gamma2': gamma2, 'beta2': beta2}
    _L0_conv_all = _L0_conv_setup()
    _L0_conv_in = {k: v for k, v in _L0_conv_all.items() if k in ('w1', 'gamma1', 'beta1', 'w2', 'gamma2', 'beta2')}
    del _L0_conv_all

    def _L1_conv_setup():
        import jax, jax.numpy as jnp
        import numpy as np
        B_, C_, H_, W_ = (16, 64, 32, 32)
        D_MODEL = C_ // 4
        D_STATE = 16
        D_CONV = 4
        EXPAND = 2
        D_INNER = EXPAND * D_MODEL
        DT_RANK = (D_MODEL + 15) // 16
        EPS = 1e-05

        def _mamba(x, in_proj_w, conv_w, conv_b, x_proj_w, dt_proj_w, dt_proj_b, A_log, D, out_proj_w):
            G, L, _ = x.shape
            xz = jnp.einsum('gld,ed->gle', x, in_proj_w)
            xi, z = jnp.split(xz, 2, axis=-1)
            xc = jax.lax.conv_general_dilated(xi.transpose(0, 2, 1), conv_w[:, None, :], window_strides=(1,), padding=[(D_CONV - 1, 0)], feature_group_count=D_INNER)
            u = jax.nn.silu(xc.transpose(0, 2, 1) + conv_b)
            x_dbl = jnp.einsum('gld,ed->gle', u, x_proj_w)
            dt, Bm, Cm = jnp.split(x_dbl, [DT_RANK, DT_RANK + D_STATE], axis=-1)
            delta = jax.nn.softplus(jnp.einsum('glr,dr->gld', dt, dt_proj_w) + dt_proj_b)
            A = -jnp.exp(A_log)

            def step(h, inputs):
                d_t, u_t, B_t, C_t = inputs
                dA = jnp.exp(d_t[..., None] * A)
                h = h * dA + (d_t * u_t)[..., None] * B_t[:, None, :]
                y = jnp.einsum('gdn,gn->gd', h, C_t)
                return (h, y)
            h0 = jnp.zeros((G, D_INNER, D_STATE), x.dtype)
            xs = (delta.transpose(1, 0, 2), u.transpose(1, 0, 2), Bm.transpose(1, 0, 2), Cm.transpose(1, 0, 2))
            _, ys = jax.lax.scan(step, h0, xs)
            y = ys.transpose(1, 0, 2) + u * D
            y = y * jax.nn.silu(z)
            return jnp.einsum('gld,ed->gle', y, out_proj_w)
        key = jax.random.key(seed)
        ks = jax.random.split(key, 8)

        def n(k, shape, scale=0.02):
            return jax.random.normal(k, shape, dtype=jnp.float32) * scale
        A = jnp.broadcast_to(jnp.arange(1, D_STATE + 1, dtype=jnp.float32), (D_INNER, D_STATE))
        return {'input': jax.random.normal(ks[0], (B_, C_, H_, W_), dtype=jnp.float32), 'ln_g': jnp.ones((C_,), jnp.float32), 'ln_b': jnp.zeros((C_,), jnp.float32), 'in_proj_w': n(ks[1], (2 * D_INNER, D_MODEL)), 'conv_w': n(ks[2], (D_INNER, D_CONV), 0.1), 'conv_b': jnp.zeros((D_INNER,), jnp.float32), 'x_proj_w': n(ks[3], (DT_RANK + 2 * D_STATE, D_INNER)), 'dt_proj_w': n(ks[4], (D_INNER, DT_RANK), 0.5), 'dt_proj_b': jnp.full((D_INNER,), -4.6, jnp.float32), 'A_log': jnp.log(A), 'D': jnp.ones((D_INNER,), jnp.float32), 'out_proj_w': n(ks[5], (D_MODEL, D_INNER))}
    _L1_conv_all = _L1_conv_setup()
    _L1_conv_in = {k: v for k, v in _L1_conv_all.items() if k in ('ln_g', 'ln_b', 'in_proj_w', 'conv_w', 'conv_b', 'x_proj_w', 'dt_proj_w', 'dt_proj_b', 'A_log', 'D', 'out_proj_w')}
    del _L1_conv_all

    def _L2_conv_setup():
        import jax, jax.numpy as jnp
        import numpy as np
        B, CIN, H, W = (4, 64, 128, 128)
        G, CI, COUT = (32, 4, 64)
        key = jax.random.key(seed)
        ks = jax.random.split(key, 7)
        s = 0.05
        return {'x': jax.random.normal(ks[0], (B, CIN, H, W), dtype=jnp.float32), 'W1': jax.random.normal(ks[1], (G, CI, CIN), dtype=jnp.float32) * s, 'b1': jax.random.normal(ks[2], (G, CI), dtype=jnp.float32) * s, 'W2': jax.random.normal(ks[3], (G, CI, CI, 3, 3), dtype=jnp.float32) * s, 'b2': jax.random.normal(ks[4], (G, CI), dtype=jnp.float32) * s, 'W3': jax.random.normal(ks[5], (G, COUT, CI), dtype=jnp.float32) * s, 'b3': jax.random.normal(ks[6], (G, COUT), dtype=jnp.float32) * s}
    _L2_conv_all = _L2_conv_setup()
    _L2_conv_in = {k: v for k, v in _L2_conv_all.items() if k in ('W1', 'b1', 'W2', 'b2', 'W3', 'b3')}
    del _L2_conv_all

    def _L3_conv_setup():
        import jax, jax.numpy as jnp
        import numpy as np
        from jax import lax
        B, C, H, W = (8, 64, 64, 64)
        KW = 9
        PW = (KW - 1) // 2

        def _make_kernel(key):
            std = float(np.sqrt(2.0 / (C * KW * C)))
            return jax.random.normal(key, (KW, C, C), dtype=jnp.float32) * std

        def _row_conv(y, K):
            return lax.conv_general_dilated(y, K, window_strides=(1,), padding=[(PW, PW)], dimension_numbers=('NWC', 'WIO', 'NWC'))

        def _dir_scan(x, K, reverse):
            if reverse:
                x = x[:, ::-1]

            def step(prev, cur):
                new = cur + jax.nn.relu(_row_conv(prev, K))
                return (new, new)
            first = x[:, 0]
            _, rest = lax.scan(step, first, jnp.moveaxis(x[:, 1:], 1, 0))
            out = jnp.concatenate([first[:, None], jnp.moveaxis(rest, 0, 1)], axis=1)
            if reverse:
                out = out[:, ::-1]
            return out
        key = jax.random.key(seed)
        kx, k1, k2, k3, k4 = jax.random.split(key, 5)
        x = jax.random.normal(kx, (B, C, H, W), dtype=jnp.float32)
        return {'x': x, 'k_td': _make_kernel(k1), 'k_dt': _make_kernel(k2), 'k_lr': _make_kernel(k3), 'k_rl': _make_kernel(k4)}
    _L3_conv_all = _L3_conv_setup()
    _L3_conv_in = {k: v for k, v in _L3_conv_all.items() if k in ('k_td', 'k_dt', 'k_lr', 'k_rl')}
    del _L3_conv_all
    return {'x': x, 'L0_conv_w1': _L0_conv_in['w1'], 'L0_conv_gamma1': _L0_conv_in['gamma1'], 'L0_conv_beta1': _L0_conv_in['beta1'], 'L0_conv_w2': _L0_conv_in['w2'], 'L0_conv_gamma2': _L0_conv_in['gamma2'], 'L0_conv_beta2': _L0_conv_in['beta2'], 'L1_conv_ln_g': _L1_conv_in['ln_g'], 'L1_conv_ln_b': _L1_conv_in['ln_b'], 'L1_conv_in_proj_w': _L1_conv_in['in_proj_w'], 'L1_conv_conv_w': _L1_conv_in['conv_w'], 'L1_conv_conv_b': _L1_conv_in['conv_b'], 'L1_conv_x_proj_w': _L1_conv_in['x_proj_w'], 'L1_conv_dt_proj_w': _L1_conv_in['dt_proj_w'], 'L1_conv_dt_proj_b': _L1_conv_in['dt_proj_b'], 'L1_conv_A_log': _L1_conv_in['A_log'], 'L1_conv_D': _L1_conv_in['D'], 'L1_conv_out_proj_w': _L1_conv_in['out_proj_w'], 'L2_conv_W1': _L2_conv_in['W1'], 'L2_conv_b1': _L2_conv_in['b1'], 'L2_conv_W2': _L2_conv_in['W2'], 'L2_conv_b2': _L2_conv_in['b2'], 'L2_conv_W3': _L2_conv_in['W3'], 'L2_conv_b3': _L2_conv_in['b3'], 'L3_conv_k_td': _L3_conv_in['k_td'], 'L3_conv_k_dt': _L3_conv_in['k_dt'], 'L3_conv_k_lr': _L3_conv_in['k_lr'], 'L3_conv_k_rl': _L3_conv_in['k_rl']}

def reference(x, L0_conv_w1, L0_conv_gamma1, L0_conv_beta1, L0_conv_w2, L0_conv_gamma2, L0_conv_beta2, L1_conv_ln_g, L1_conv_ln_b, L1_conv_in_proj_w, L1_conv_conv_w, L1_conv_conv_b, L1_conv_x_proj_w, L1_conv_dt_proj_w, L1_conv_dt_proj_b, L1_conv_A_log, L1_conv_D, L1_conv_out_proj_w, L2_conv_W1, L2_conv_b1, L2_conv_W2, L2_conv_b2, L2_conv_W3, L2_conv_b3, L3_conv_k_td, L3_conv_k_dt, L3_conv_k_lr, L3_conv_k_rl):
    import jax
    import jax.numpy as jnp

    def _L0_conv_ref(x, w1, gamma1, beta1, w2, gamma2, beta2):
        import jax, jax.numpy as jnp
        import numpy as np
        from jax import lax
        EPS = 1e-05

        def _conv3x3(x, w):
            return lax.conv_general_dilated(x, w, window_strides=(1, 1), padding=((1, 1), (1, 1)), dimension_numbers=('NCHW', 'OIHW', 'NCHW'))

        def _batchnorm(y, gamma, beta):
            mean = jnp.mean(y, axis=(0, 2, 3), keepdims=True)
            var = jnp.var(y, axis=(0, 2, 3), keepdims=True)
            inv = lax.rsqrt(var + EPS)
            return (y - mean) * inv * gamma[None, :, None, None] + beta[None, :, None, None]
        w1b = w1 + lax.stop_gradient(jnp.sign(w1) - w1)
        w2b = w2 + lax.stop_gradient(jnp.sign(w2) - w2)
        out = jax.nn.relu(_batchnorm(_conv3x3(x, w1b), gamma1, beta1))
        out = _batchnorm(_conv3x3(out, w2b), gamma2, beta2)
        out = out + x
        return jax.nn.relu(out)

    def _L1_conv_ref(input, ln_g, ln_b, in_proj_w, conv_w, conv_b, x_proj_w, dt_proj_w, dt_proj_b, A_log, D, out_proj_w):
        import jax, jax.numpy as jnp
        import numpy as np
        B_, C_, H_, W_ = (16, 64, 32, 32)
        D_MODEL = C_ // 4
        D_STATE = 16
        D_CONV = 4
        EXPAND = 2
        D_INNER = EXPAND * D_MODEL
        DT_RANK = (D_MODEL + 15) // 16
        EPS = 1e-05

        def _mamba(x, in_proj_w, conv_w, conv_b, x_proj_w, dt_proj_w, dt_proj_b, A_log, D, out_proj_w):
            G, L, _ = x.shape
            xz = jnp.einsum('gld,ed->gle', x, in_proj_w)
            xi, z = jnp.split(xz, 2, axis=-1)
            xc = jax.lax.conv_general_dilated(xi.transpose(0, 2, 1), conv_w[:, None, :], window_strides=(1,), padding=[(D_CONV - 1, 0)], feature_group_count=D_INNER)
            u = jax.nn.silu(xc.transpose(0, 2, 1) + conv_b)
            x_dbl = jnp.einsum('gld,ed->gle', u, x_proj_w)
            dt, Bm, Cm = jnp.split(x_dbl, [DT_RANK, DT_RANK + D_STATE], axis=-1)
            delta = jax.nn.softplus(jnp.einsum('glr,dr->gld', dt, dt_proj_w) + dt_proj_b)
            A = -jnp.exp(A_log)

            def step(h, inputs):
                d_t, u_t, B_t, C_t = inputs
                dA = jnp.exp(d_t[..., None] * A)
                h = h * dA + (d_t * u_t)[..., None] * B_t[:, None, :]
                y = jnp.einsum('gdn,gn->gd', h, C_t)
                return (h, y)
            h0 = jnp.zeros((G, D_INNER, D_STATE), x.dtype)
            xs = (delta.transpose(1, 0, 2), u.transpose(1, 0, 2), Bm.transpose(1, 0, 2), Cm.transpose(1, 0, 2))
            _, ys = jax.lax.scan(step, h0, xs)
            y = ys.transpose(1, 0, 2) + u * D
            y = y * jax.nn.silu(z)
            return jnp.einsum('gld,ed->gle', y, out_proj_w)
        B, C, H, W = input.shape
        L = H * W
        xf = input.reshape(B, C, L).transpose(0, 2, 1)
        mu = xf.mean(-1, keepdims=True)
        var = ((xf - mu) ** 2).mean(-1, keepdims=True)
        xn = (xf - mu) / jnp.sqrt(var + EPS) * ln_g + ln_b
        chunks = xn.reshape(B, L, 4, C // 4).transpose(2, 0, 1, 3).reshape(4 * B, L, C // 4)
        y = chunks + _mamba(chunks, in_proj_w, conv_w, conv_b, x_proj_w, dt_proj_w, dt_proj_b, A_log, D, out_proj_w)
        out = y.reshape(4, B, L, C // 4).transpose(1, 2, 0, 3).reshape(B, L, C)
        return out.transpose(0, 2, 1).reshape(B, C, H, W)

    def _L2_conv_ref(x, W1, b1, W2, b2, W3, b3):
        import jax, jax.numpy as jnp
        import numpy as np
        B, CIN, H, W = (4, 64, 128, 128)
        G, CI, COUT = (32, 4, 64)
        g, ci, cin = W1.shape
        b, _, h, w = x.shape
        t = jnp.einsum('gic,bchw->bgihw', W1, x) + b1[None, :, :, None, None]
        t = t.reshape(b, g * ci, h, w)
        k = W2.reshape(g * ci, ci, 3, 3)
        t = jax.lax.conv_general_dilated(t, k, window_strides=(1, 1), padding='SAME', dimension_numbers=('NCHW', 'OIHW', 'NCHW'), feature_group_count=g)
        t = t + b2.reshape(1, g * ci, 1, 1)
        t = t.reshape(b, g, ci, h, w)
        out = jnp.einsum('goi,bgihw->bohw', W3, t) + b3.sum(axis=0)[None, :, None, None]
        out = out + x
        return out

    def _L3_conv_ref(x, k_td, k_dt, k_lr, k_rl):
        import jax, jax.numpy as jnp
        import numpy as np
        from jax import lax
        B, C, H, W = (8, 64, 64, 64)
        KW = 9
        PW = (KW - 1) // 2

        def _make_kernel(key):
            std = float(np.sqrt(2.0 / (C * KW * C)))
            return jax.random.normal(key, (KW, C, C), dtype=jnp.float32) * std

        def _row_conv(y, K):
            return lax.conv_general_dilated(y, K, window_strides=(1,), padding=[(PW, PW)], dimension_numbers=('NWC', 'WIO', 'NWC'))

        def _dir_scan(x, K, reverse):
            if reverse:
                x = x[:, ::-1]

            def step(prev, cur):
                new = cur + jax.nn.relu(_row_conv(prev, K))
                return (new, new)
            first = x[:, 0]
            _, rest = lax.scan(step, first, jnp.moveaxis(x[:, 1:], 1, 0))
            out = jnp.concatenate([first[:, None], jnp.moveaxis(rest, 0, 1)], axis=1)
            if reverse:
                out = out[:, ::-1]
            return out
        y = jnp.transpose(x, (0, 2, 3, 1))
        y = _dir_scan(y, k_td, reverse=False)
        y = _dir_scan(y, k_dt, reverse=True)
        yt = jnp.swapaxes(y, 1, 2)
        yt = _dir_scan(yt, k_lr, reverse=False)
        yt = _dir_scan(yt, k_rl, reverse=True)
        y = jnp.swapaxes(yt, 1, 2)
        return jnp.transpose(y, (0, 3, 1, 2))

    def _gn(v, G=32, eps=1e-05):
        B_, C_, H_, W_ = v.shape
        g = v.reshape(B_, G, C_ // G, H_, W_)
        m = jnp.mean(g, axis=(2, 3, 4), keepdims=True)
        s = jnp.var(g, axis=(2, 3, 4), keepdims=True)
        return ((g - m) / jnp.sqrt(s + eps)).reshape(v.shape)

    def _ln_c(v, eps=1e-06):
        m = jnp.mean(v, axis=1, keepdims=True)
        s = jnp.var(v, axis=1, keepdims=True)
        return (v - m) / jnp.sqrt(s + eps)

    def _ln_t(v, eps=1e-05):
        m = jnp.mean(v, axis=-1, keepdims=True)
        s = jnp.var(v, axis=-1, keepdims=True)
        return (v - m) / jnp.sqrt(s + eps)

    def _to_tokens(v):
        B_, C_, H_, W_ = v.shape
        return v.reshape(B_, C_, H_ * W_).transpose(0, 2, 1)

    def _from_tokens(t, like):
        B_, C_, H_, W_ = like.shape
        return t.transpose(0, 2, 1).reshape(B_, C_, H_, W_)
    x = _L0_conv_ref(x, L0_conv_w1, L0_conv_gamma1, L0_conv_beta1, L0_conv_w2, L0_conv_gamma2, L0_conv_beta2)
    x = _L1_conv_ref(x, L1_conv_ln_g, L1_conv_ln_b, L1_conv_in_proj_w, L1_conv_conv_w, L1_conv_conv_b, L1_conv_x_proj_w, L1_conv_dt_proj_w, L1_conv_dt_proj_b, L1_conv_A_log, L1_conv_D, L1_conv_out_proj_w)
    x = _L2_conv_ref(x, L2_conv_W1, L2_conv_b1, L2_conv_W2, L2_conv_b2, L2_conv_W3, L2_conv_b3)
    x = _L3_conv_ref(x, L3_conv_k_td, L3_conv_k_dt, L3_conv_k_lr, L3_conv_k_rl)
    return x

_drawn_inputs = setup_inputs


def setup_inputs(seed=0):
    import zlib

    import numpy as np

    out = dict(_drawn_inputs(seed))
    spreads = {'L0_conv_gamma1': (1.0, 0.2),
     'L0_conv_beta1': (0.0, 0.1),
     'L0_conv_gamma2': (1.0, 0.2),
     'L0_conv_beta2': (0.0, 0.1),
     'L1_conv_ln_g': (1.0, 0.2),
     'L1_conv_ln_b': (0.0, 0.1),
     'L1_conv_conv_b': (0.0, 0.8),
     'L1_conv_dt_proj_b': (-4.599999904632568, 0.6),
     'L1_conv_D': (1.0, 0.6)}
    factors = {'L1_conv_in_proj_w': 8.0,
     'L1_conv_conv_w': 8.0,
     'L1_conv_x_proj_w': 8.0,
     'L1_conv_dt_proj_w': 8.0,
     'L1_conv_A_log': 8.0,
     'L1_conv_out_proj_w': 8.0,
     'L2_conv_b1': 6.642,
     'L2_conv_b2': 3.629}
    for name, (base, spread) in spreads.items():
        noise = np.random.default_rng([zlib.crc32(name.encode()), seed]).standard_normal(out[name].shape)
        drawn = base * np.exp(spread * noise) if base else spread * noise
        out[name] = jnp.asarray(drawn.astype(out[name].dtype))
    for name, factor in factors.items():
        out[name] = (out[name] * factor).astype(out[name].dtype)
    return out
```

```python
from contextlib import ExitStack

import concourse.bass as bass
from concourse import mybir

ALU = mybir.AluOpType
ACT = mybir.ActivationFunctionType
F32 = mybir.dt.float32
BF16 = mybir.dt.bfloat16

P = 128
C = 64
HC = 4
DI = 32
NS = 16
H = W = 56
HW = H * W
HALF = W // 2
PIX = H * HALF
KW = 9
KS = 5
PADS = 2
EPS = 1e-5

PACK_A = [("conv1", 6 * P), ("conv2", 6 * P), ("halves", P), ("vecs", 5)]
PACK_C = [("conv_in", 2 * P), ("gate_in", 2 * P), ("taps", 4 * P), ("spread_bc", 2 * HC * P),
          ("select_d", 4 * P), ("reduce_n", 4 * DI), ("proj_out", C), ("residual", 2 * C),
          ("centre", P), ("average", P), ("dt_rows", 2 * P), ("vecs", 6), ("a_log", 4)]
PACK_D = [("w1b1", C + 1), ("w2", 9 * P), ("w3", C), ("ident", C), ("b3", C), ("ones", 1), ("b2", 1)]
PACK_S = [("scan", 4 * KS * P)]


def columns(pack):
    at, out = 0, {}
    for name, n in pack:
        out[name] = (at, at + n)
        at += n
    return out, at


def build(nc, x, pack_a, pack_c, pack_d, pack_s, out):
    N = x.shape[0]
    PAIRS = N // 2
    QT = 4
    QR = HALF // QT
    QN = QR * W
    T = 448
    TR = T // W
    KT = HW // T
    ST = 2 * KT
    UN = HC * 4
    GRP = N // 2
    CH = GRP // 2

    ca, na = columns(PACK_A)
    cc, ncc = columns(PACK_C)
    cd, nd = columns(PACK_D)
    cs, ns = columns(PACK_S)

    y1 = nc.dram_tensor("y1_pairs", (N, P, PIX), F32, kind="Internal").ap()
    y2 = nc.dram_tensor("y2_nchw", (N, C, H, W), F32, kind="Internal").ap()
    x3 = nc.dram_tensor("x3_column_pairs", (N, P, H, HALF + 1), F32, kind="Internal").ap()

    with ExitStack() as ctx:
        def sem(name):
            return ctx.enter_context(nc.semaphore(name))

        def sb(stack, name, shape, dt=F32):
            return stack.enter_context(nc.sbuf_tensor(name, shape, dt))

        ps = ctx.enter_context(nc.psum_tensor("ps", [P, 8, 512], F32))
        bn = sb(ctx, "bn", [P, 24])

        with ExitStack() as m:
            wa = sb(m, "wa", [P, na])
            signs = sb(m, "signs", [P, 2, 6, P])
            xpad = sb(m, "xpad", [P, 2, HALF + 1, W + 2])
            yin = sb(m, "yin", [P, 2, PIX])
            yout = sb(m, "yout", [P, 2, PIX])
            stats = sb(m, "stats", [P, N * QT, 6])
        with ExitStack() as m:
            wc = sb(m, "wc", [P, ncc])
            wtap = sb(m, "wtap", [P, 2, 4, P])
            wdt = sb(m, "wdt", [P, P])
            seld = sb(m, "seld", [P, 4, P], BF16)
            nega = sb(m, "nega", [P, 4])
            lnx = sb(m, "lnx", [P, T])
            lny = sb(m, "lny", [P, T])
            xsum = sb(m, "xsum", [P, T])
            xres = sb(m, "xres", [P, T])
            xcen = sb(m, "xcen", [P, T])
            xsq = sb(m, "xsq", [P, T])
            xvar = sb(m, "xvar", [P, T])
            xrstd = sb(m, "xrstd", [P, T])
            xg = sb(m, "xg", [P, T])
            xn = sb(m, "xn", [P, 3 + HW])
            u = sb(m, "u", [P, 4, T])
            sz = sb(m, "sz", [P, 4, T])
            dabs = sb(m, "dabs", [P, T])
            drelu = sb(m, "drelu", [P, T])
            dexp = sb(m, "dexp", [P, T])
            dln = sb(m, "dln", [P, T])
            dq = sb(m, "dq", [P, T])
            ds1 = sb(m, "ds1", [P, T])
            ds2 = sb(m, "ds2", [P, T])
            dlt = sb(m, "dlt", [P, 2, T])
            rest = sb(m, "rest", [P, 2, T])
            parts = sb(m, "parts", [P, 2, 3, T], BF16)
            stack = sb(m, "stack", [96, 2, 2, HC, T], BF16)
            bsp = sb(m, "bsp", [P, 2, 2 * HC, T])
            da = sb(m, "da", [P, 4, T])
            dbu = sb(m, "dbu", [P, 2, T])
            hs = sb(m, "hs", [P, UN, T])
            prod = sb(m, "prod", [P, 8, T])
            yd = sb(m, "yd", [P, T])
            yg = sb(m, "yg", [P, T])
            otile = sb(m, "otile", [P, 2, TR, HALF + 1])
        with ExitStack() as m:
            wd = sb(m, "wd", [P, nd])
            ws = sb(m, "ws", [P, ns])
            rmix = sb(m, "rmix", [P, 9, C + 1])
            lw = sb(m, "lw", [P, 6, P])
            bt = sb(m, "bt", [P, 16])
            bmap = sb(m, "bmap", [P, H, HALF])
            xpad3 = sb(m, "xpad3", [P, 2, H + 2, HALF + 1])
            R = sb(m, "R", [P, GRP, PIX])
            pv = sb(m, "pv", [P, 2, 4, CH, HALF + 2 * PADS])

        phase_done = sem("phase_done")
        pack_in = sem("pack_in")

        def barrier(e, k):
            e.drain().then_inc(phase_done, 1)
            e.wait_ge(phase_done, 5 * k)

        def conv_sems(s):
            return {n: sem(f"{s}_{n}") for n in (
                "weights_ready", "in_loaded0", "in_loaded1", "padded", "conv_done", "psum_free",
                "stored0", "stored1", "out_ready", "stat_chain", "stat_mean", "stat_halves",
                "stat_var", "stat_rstd")}
        sa, sbm = conv_sems("a"), conv_sems("b")
        pads_zeroed = sem("pads_zeroed")

        S = {n: sem("c_" + n) for n in (
            "gates", "zeroed", "prep", "wdt_mm", "ready", "ln_loaded", "x_summed", "x_relu", "centred",
            "squared", "var_copied", "rstd", "scaled", "xn_ready",
            "tmp_done", "u_ready", "sz_ready", "d_abs", "d_relu", "d_exp", "d_ln", "d_q",
            "d_s1", "d_s2", "d_min", "delta", "delta_u", "split_chain", "split0", "split1", "stacked0", "stacked1",
            "bc_ready", "d_spread", "du_spread", "exp_done", "dbu_done", "scan_done", "prod_done",
            "y_summed", "y_d", "y_gated", "out_mm", "out_evac", "out_stored0", "out_stored1")}

        D = {n: sem("d_" + n) for n in (
            "loaded0", "loaded1", "zeroed", "gates", "prep_mm", "prep_v", "bias_ready", "conv_done", "evacuated",
            "mm0", "mm1", "row0", "row1", "copied0", "copied1", "stored")}

        def vec_a(i):
            return wa[:, ca["vecs"][0] + i:ca["vecs"][0] + i + 1]

        def vec_c(i):
            return wc[:, cc["vecs"][0] + i:cc["vecs"][0] + i + 1]

        def wcs(name, i, n):
            a = cc[name][0] + i * n
            return wc[:, a:a + n]

        SCALE1, SHIFT1, SCALE2, SHIFT2 = 10, 11, 12, 13

        def col(i, n=1):
            return bn[:, i:i + n]

        def conv_pe(pe, s, layer, ready, per_image):
            pe.wait_ge(s["weights_ready"], 1)
            with pe.Fori(0, PAIRS) as i:
                for b in range(2):
                    pe.wait_ge(ready[b], per_image * (i + 1))
                    for q in range(QT):
                        pe.wait_ge(s["psum_free"], i * 8 + b * QT + q + 1)
                        for kx in range(3):
                            for ab in range(2):
                                mm = pe.matmul(ps[:, b * QT + q, 0:QN], signs[:, layer, kx * 2 + ab, :],
                                               xpad[:, b, q * QR + ab:q * QR + ab + QR, kx:kx + W],
                                               start=(kx + ab == 0), stop=(kx + ab == 3))
                        mm.then_inc(s["conv_done"], 1)

        def conv_dve(v, s, i, b):
            for q in range(QT):
                v.wait_ge(s["conv_done"], i * 8 + b * QT + q + 1)
                if q == 0:
                    v.wait_ge(s[f"stored{b}"], i * s["store_steps"])
                v.tensor_copy(yout[:, b, q * QN:(q + 1) * QN], ps[:, b * QT + q, 0:QN]).then_inc(s["out_ready"], 1)
                v.bn_stats(stats[:, i * 8 + (b * QT + q), :], ps[:, b * QT + q, 0:QN]).then_inc(s["psum_free"], 1)

        def batch_stats(v, s, g0, scale, shift):
            n = [0]

            def step(ins):
                n[0] += 1
                ins.then_inc(s["stat_chain"], 1)
                v.wait_ge(s["stat_chain"], n[0])

            v.wait_ge(s["psum_free"], 8 * PAIRS + 8)
            step(v.bn_aggr(col(0, 2), stats[:, :, :]))
            step(v.tensor_copy(col(2), col(0)))
            v.scalar_tensor_tensor(col(3), col(0), col(0), col(1), ALU.mult, ALU.add).then_inc(s["stat_mean"], 1)
            v.wait_ge(s["stat_halves"], 1)
            step(v.tensor_copy(col(4, 2), ps[:, 0, 0:2]))
            step(v.tensor_scalar(col(6), col(4), -1.0, None, ALU.mult))
            v.scalar_tensor_tensor(col(7), col(4), col(6), col(5), ALU.mult, ALU.add).then_inc(s["stat_var"], 1)
            v.wait_ge(s["stat_rstd"], 2)
            step(v.tensor_scalar(col(7), col(7), EPS, -0.5, ALU.add, ALU.mult))
            step(v.tensor_tensor(col(9), col(8), col(8), ALU.mult))
            step(v.tensor_scalar(col(9), col(9), col(7), 1.5, ALU.mult, ALU.add))
            step(v.tensor_tensor(col(8), col(8), col(9), ALU.mult))
            step(v.tensor_tensor(col(scale), vec_a(g0), col(8), ALU.mult))
            step(v.scalar_tensor_tensor(col(shift), col(scale), col(6), vec_a(g0 + 1), ALU.mult, ALU.add))

        def rstd_act(a, s):
            a.wait_ge(s["stat_var"], 1)
            a.activation(col(14), col(7), ACT.Ln, bias=vec_a(4)).then_inc(s["stat_rstd"], 1)
            a.wait_ge(s["stat_rstd"], 1)
            a.activation(col(8), col(14), ACT.Exp, scale=-0.5).then_inc(s["stat_rstd"], 1)

        def halves_pe(pe, s):
            pe.wait_ge(s["stat_mean"], 1)
            pe.matmul(ps[:, 0, 0:2], wa[:, ca["halves"][0]:ca["halves"][1]], col(2, 2),
                      start=True, stop=True).then_inc(s["stat_halves"], 1)

        sa["store_steps"], sbm["store_steps"] = 16, 32

        UB = [0, 1, 2, 0, 1, 2, 0, 1, 2, 3, 0, 1, 2, 3]
        assert len(UB) == ST
        BASE = 6 * 2 + 11
        TASKS = ["u", "z", "dt", "bc0", "bc1", "lnc", "bc2", "lnv", "bc3", "bc4", "bc5", "bc6", "bc7"]
        AT = {}
        n_tmp = 0
        for t in range(ST):
            for name in TASKS:
                if name.startswith("ln") and not (t == 0 or t >= 8):
                    continue
                AT[(t, name)] = n_tmp
                n_tmp += 1
        TMP = n_tmp
        assert TMP % 2 == 0
        D_BANK, DU_BANK, TMP_BANK, Y_BANK, O_BANK = 0, 2, 4, 6, 7

        class Step:
            def __init__(self, p, t):
                self.p, self.t, self.ahead = p, t, False
                self.tile = p * ST + t
                nt = (t + 1) % ST
                self.next_s, self.next_k = nt // KT, nt % KT
                self.next_pair = p + (t + 1) // ST
                self.next_u = UB[nt]
                self.par = (t + 1) % 2
                self.has_ln = t == 0 or t >= 8
                self.ln = p * KT + 6 if t == 0 else (p + 1) * KT + (t - 8)
                self.ln_k = 6 if t == 0 else t - 8
                self.ln_pair = p if t == 0 else (p + 1) % PAIRS
                self.ln_out = p * ST if t == 0 else p * ST + t

            def tmp(self, name):
                i = AT[(self.t, name)]
                return self.p * TMP + (i + BASE), (i + BASE) % 2

        class Ahead:
            def __init__(self, k=None):
                self.par, self.next_s, self.next_k, self.next_u, self.next_pair = 0, 0, 0, 0, 0
                self.tile, self.ahead = -1, True
                self.ln, self.ln_k, self.ln_pair, self.ln_out = k, k, 0, 0
                self.k = k

            def tmp(self, name):
                i = (self.k * 2 + (name == "lnv")) if name.startswith("ln") else \
                    12 + [n for n in TASKS if not n.startswith("ln")].index(name)
                return i, i % 2

        def wait_bank(pe, st, name):
            order = [n for n in TASKS if not n.startswith("ln") or (not st.ahead and st.has_ln)]
            tile, ln = st.tile, st.ln
            if st.ahead and name.startswith("ln"):
                if st.k == 0:
                    return
                back = name
                ln = st.ln - 1
            else:
                i = order.index(name) - 2
                if i >= 0:
                    back = order[i]
                elif st.ahead:
                    back, ln = ("lnc", "lnv")[i + 2], 5
                else:
                    back, tile = order[i], tile - 1
            if back.startswith("bc"):
                pe.wait_ge(S["bc_ready"], (tile + 1) * 8 + int(back[2:]) + 1)
            elif back.startswith("ln"):
                pe.wait_ge(S["squared" if back == "lnc" else "var_copied"], ln + 1)
            else:
                pe.wait_ge(S[{"u": "u_ready", "z": "sz_ready", "dt": "d_relu"}[back]], tile + 2)

        def tmp_pe(pe, st, name, emit):
            n, bank = st.tmp(name)
            wait_bank(pe, st, name)
            emit(ps[:, TMP_BANK + bank, 0:T]).then_inc(S["tmp_done"], 1)

        def pe_task(pe, st, name):
            if name == "u":
                pe.wait_ge(S["xn_ready"], st.next_pair * KT + st.next_k + 1)

                def emit(o):
                    for k in range(4):
                        a = st.next_k * T + k
                        mm = pe.matmul(o, wtap[:, st.next_s, k, :], xn[:, a:a + T], start=(k == 0), stop=(k == 3))
                    return mm
            elif name == "z":
                def emit(o):
                    a = st.next_k * T + 3
                    return pe.matmul(o, wcs("gate_in", st.next_s, P), xn[:, a:a + T], start=True, stop=True)
            elif name == "dt":
                pe.wait_ge(S["u_ready"], st.tile + 2)

                def emit(o):
                    return pe.matmul(o, wdt[:, :], u[:, st.next_u, :], start=True, stop=True)
            elif name.startswith("bc"):
                def emit(o):
                    return pe.matmul(o, wcs("spread_bc", int(name[2:]), P), u[:, st.next_u, :], start=True, stop=True)
            elif name == "lnc":
                pe.wait_ge(S["x_relu"], st.ln + 1)

                def emit(o):
                    return pe.matmul(o, wcs("centre", 0, P), xres[:, :], start=True, stop=True)
            else:
                pe.wait_ge(S["squared"], st.ln + 1)

                def emit(o):
                    return pe.matmul(o, wcs("average", 0, P), xsq[:, :], start=True, stop=True)
            tmp_pe(pe, st, name, emit)

        def act_task(a, st, name):
            n, bank = st.tmp(name)
            src = ps[:, TMP_BANK + bank, 0:T]
            a.wait_ge(S["tmp_done"], n + 1)
            if name == "u":
                if not st.ahead:
                    a.wait_ge(S["y_gated"], st.tile)
                a.activation(u[:, st.next_u, :], src, ACT.Silu, bias=vec_c(2)).then_inc(S["u_ready"], 1)
            elif name == "z":
                a.activation(sz[:, st.next_u, :], src, ACT.Silu).then_inc(S["sz_ready"], 1)
            elif name == "dt":
                if not st.ahead:
                    a.wait_ge(S["delta"], st.tile + 1)
                a.activation(dabs[:, :], src, ACT.Abs, bias=vec_c(3)).then_inc(S["d_abs"], 1)
                a.activation(drelu[:, :], src, ACT.Relu, bias=vec_c(3)).then_inc(S["d_relu"], 1)
                a.wait_ge(S["d_abs"], st.tile + 2)
                a.activation(dexp[:, :], dabs[:, :], ACT.Exp, scale=-1.0).then_inc(S["d_exp"], 1)
                a.wait_ge(S["d_exp"], st.tile + 2)
                a.activation(dln[:, :], dexp[:, :], ACT.Ln, bias=1.0).then_inc(S["d_ln"], 1)
            elif name.startswith("bc"):
                if not st.ahead:
                    a.wait_ge(S["prod_done"], st.tile * UN + UN)
                a.copy(bsp[:, st.par, int(name[2:]), :], src).then_inc(S["bc_ready"], 1)
            elif name == "lnc":
                if not (st.ahead and st.k == 0):
                    a.wait_ge(S["scaled"], st.ln)
                a.copy(xcen[:, :], src).then_inc(S["centred"], 1)
                a.activation(xsq[:, :], src, ACT.Square).then_inc(S["squared"], 1)
            else:
                a.activation(xvar[:, :], src, ACT.Ln, bias=vec_c(5)).then_inc(S["var_copied"], 1)
                a.wait_ge(S["var_copied"], st.ln + 1)
                a.activation(xrstd[:, :], xvar[:, :], ACT.Exp, scale=-0.5).then_inc(S["rstd"], 1)

        def ln_load(sp, st):
            if not (st.ahead and st.k == 0):
                sp.wait_ge(S["x_summed"], st.ln)
            a = st.ln_k * T
            for dst, src in ((lnx, x), (lny, y2)):
                v = src.rearrange("(g n) c h w -> g (n c) (h w)", n=2)
                sp.dma_start(dst[:, :], v[st.ln_pair, :, a:a + T]).then_inc(S["ln_loaded"], 16)

        def ln_sum(v, st):
            v.wait_ge(S["ln_loaded"], (st.ln + 1) * 32)
            if not (st.ahead and st.k == 0):
                v.wait_ge(S["x_relu"], st.ln)
            v.scalar_tensor_tensor(xsum[:, :], lny[:, :], col(SCALE2), lnx[:, :], ALU.mult, ALU.add)\
                .then_inc(S["x_summed"], 1)

        def ln_relu(a, st):
            a.wait_ge(S["x_summed"], st.ln + 1)
            if not (st.ahead and st.k == 0):
                a.wait_ge(S["centred"], st.ln)
            a.activation(xres[:, :], xsum[:, :], ACT.Relu, bias=col(SHIFT2)).then_inc(S["x_relu"], 1)

        def ln_scale(v, st):
            v.wait_ge(S["rstd"], st.ln + 1)
            if not (st.ahead and st.k == 0):
                v.wait_ge(S["xn_ready"], st.ln)
            v.scalar_tensor_tensor(xg[:, :], xcen[:, :], vec_c(0), xrstd[:, :], ALU.mult, ALU.mult)\
                .then_inc(S["scaled"], 1)

        def ln_shift(a, st):
            a.wait_ge(S["scaled"], st.ln + 1)
            if not st.ahead:
                a.wait_ge(S["out_mm"], st.ln_out + 1)
            k = st.ln_k * T + 3
            a.activation(xn[:, k:k + T], xg[:, :], ACT.Identity, bias=vec_c(1)).then_inc(S["xn_ready"], 1)

        def delta_q(v, st):
            v.wait_ge(S["d_exp"], st.tile + 2)
            v.tensor_scalar(dq[:, :], dexp[:, :], 1.0, -1.0, ALU.add, ALU.add).then_inc(S["d_q"], 1)

        def delta_s(g, st):
            if not st.ahead:
                g.wait_ge(S["delta"], st.tile + 1)
            g.wait_ge(S["d_q"], st.tile + 2)
            g.tensor_tensor(ds2[:, :], dexp[:, :], dq[:, :], ALU.subtract).then_inc(S["d_s2"], 1)
            g.wait_ge(S["d_s2"], st.tile + 2)
            g.wait_ge(S["d_ln"], st.tile + 2)
            g.tensor_tensor(ds1[:, :], dln[:, :], ds2[:, :], ALU.add).then_inc(S["d_s1"], 1)

        def delta_sum(v, st):
            v.wait_ge(S["d_s1"], st.tile + 2)
            v.tensor_tensor(ds1[:, :], ds1[:, :], dexp[:, :], ALU.min).then_inc(S["d_min"], 1)
            if not st.ahead:
                v.wait_ge(S["delta_u"], st.tile + 1)
            v.wait_ge(S["d_min"], st.tile + 2)
            v.wait_ge(S["d_relu"], st.tile + 2)
            v.tensor_tensor(dlt[:, 0, :], ds1[:, :], drelu[:, :], ALU.add).then_inc(S["delta"], 1)

        def delta_times_u(g, st):
            if not st.ahead:
                g.wait_ge(S["split1"], st.tile + 1)
            g.wait_ge(S["delta"], st.tile + 2)
            g.wait_ge(S["u_ready"], st.tile + 2)
            g.tensor_tensor(dlt[:, 1, :], dlt[:, 0, :], u[:, st.next_u, :], ALU.mult).then_inc(S["delta_u"], 1)

        def split(v, st, i):
            v.wait_ge(S["delta"] if i == 0 else S["delta_u"], st.tile + 2)
            if not st.ahead:
                v.wait_ge(S[f"stacked{i}"], (st.tile + 1) * 192)
            n = (st.tile + 1) * 6 + 3 * i
            v.tensor_copy(parts[:, i, 0, :], dlt[:, i, :]).then_inc(S["split_chain"], 1)
            v.wait_ge(S["split_chain"], n + 1)
            v.tensor_tensor(rest[:, i, :], dlt[:, i, :], parts[:, i, 0, :], ALU.subtract).then_inc(S["split_chain"], 1)
            v.wait_ge(S["split_chain"], n + 2)
            v.tensor_copy(parts[:, i, 1, :], rest[:, i, :]).then_inc(S["split_chain"], 1)
            v.wait_ge(S["split_chain"], n + 3)
            v.tensor_tensor(parts[:, i, 2, :], rest[:, i, :], parts[:, i, 1, :], ALU.subtract)\
                .then_inc(S[f"split{i}"], 1)

        def stack_parts(sp, st, i):
            if not st.ahead:
                sp.wait_ge(S["d_spread"] if i == 0 else S["du_spread"], st.tile * UN)
                sp.sem_inc(S["gates"], 1)
            sp.wait_ge(S[f"split{i}"], st.tile + 2)
            for part in range(3):
                for c in range(HC):
                    sp.dma_start(stack[32 * part:32 * part + 32, st.par, i, c, :],
                                 parts[32 * c:32 * c + 32, i, part, :]).then_inc(S[f"stacked{i}"], 16)

        def spread(pe, st, j):
            b, c = j // HC, j % HC
            n = st.tile * UN + j
            if j == 0:
                pe.wait_ge(S["stacked0"], (st.tile + 1) * 192)
                pe.wait_ge(S["stacked1"], (st.tile + 1) * 192)
            pe.wait_ge(S["exp_done"], n + 1)
            pe.matmul(ps[:, D_BANK + j % 2, 0:T], seld[0:96, b, :], stack[:, st.t % 2, 0, c, :],
                      start=True, stop=True).then_inc(S["d_spread"], 1)
            pe.wait_ge(S["dbu_done"], n + 1)
            pe.matmul(ps[:, DU_BANK + j % 2, 0:T], seld[0:96, b, :], stack[:, st.t % 2, 1, c, :],
                      start=True, stop=True).then_inc(S["du_spread"], 1)

        def decay(a, st, j):
            n = st.tile * UN + j
            a.wait_ge(S["d_spread"], n + 1)
            a.wait_ge(S["scan_done"], n + 1)
            a.activation(da[:, j % 4, :], ps[:, D_BANK + j % 2, 0:T], ACT.Exp, scale=nega[:, j // HC:j // HC + 1])\
                .then_inc(S["exp_done"], 1)

        def drive(v, st, j):
            n = st.tile * UN + j
            v.wait_ge(S["du_spread"], n + 1)
            if j < HC:
                v.wait_ge(S["bc_ready"], st.tile * 8 + 2 * j + 1)
            v.wait_ge(S["scan_done"], n + 3)
            v.tensor_tensor(dbu[:, j % 2, :], ps[:, DU_BANK + j % 2, 0:T], bsp[:, st.t % 2, 2 * (j % HC), :],
                            ALU.mult).then_inc(S["dbu_done"], 1)

        def scan(v, st, j):
            n = st.tile * UN + j
            v.wait_ge(S["exp_done"], n + 3)
            v.wait_ge(S["dbu_done"], n + 3)
            v.wait_ge(S["prod_done"], n + 1)
            first = st.t % KT == 0
            v.tensor_tensor_scan(hs[:, j, :], da[:, j % 4, :], dbu[:, j % 2, :],
                                 0.0 if first else hs[:, j, T - 1:T], ALU.mult, ALU.add)\
                .then_inc(S["scan_done"], 1)

        def times_c(g, st, j):
            n = st.tile * UN + j
            g.wait_ge(S["scan_done"], n + 5)
            if j < HC:
                g.wait_ge(S["bc_ready"], st.tile * 8 + 2 * j + 2)
            if j % HC == 0:
                g.wait_ge(S["y_summed"], st.tile * 4 + j // HC + 3)
            g.tensor_tensor(prod[:, j % 8, :], hs[:, j, :], bsp[:, st.t % 2, 2 * (j % HC) + 1, :], ALU.mult)\
                .then_inc(S["prod_done"], 1)

        def sum_states(pe, tile, b):
            if b == 0:
                pe.wait_ge(S["y_d"], tile + 1)
            for c in range(HC):
                pe.wait_ge(S["prod_done"], tile * UN + b * HC + c + 17)
                mm = pe.matmul(ps[DI * c:DI * c + DI, Y_BANK, 0:T], wcs("reduce_n", b, DI),
                               prod[:, (b * HC + c) % 8, :], start=(b == 0), stop=(b == 3))
            mm.then_inc(S["y_summed"], 1)

        def add_du(v, tile, ub):
            v.wait_ge(S["y_summed"], tile * 4 + 8)
            v.wait_ge(S["y_gated"], tile + 1)
            v.scalar_tensor_tensor(yd[:, :], u[:, ub, :], vec_c(4), ps[:, Y_BANK, 0:T], ALU.mult, ALU.add)\
                .then_inc(S["y_d"], 1)

        def gate(g, tile, ub):
            g.wait_ge(S["y_d"], tile + 2)
            g.wait_ge(S["out_mm"], tile + 1)
            g.wait_ge(S["sz_ready"], tile + 1)
            g.tensor_tensor(yg[:, :], yd[:, :], sz[:, ub, :], ALU.mult).then_inc(S["y_gated"], 1)

        def project_out(pe, tile, s, k):
            pe.wait_ge(S["y_gated"], tile + 2)
            pe.wait_ge(S["out_evac"], tile * 2 + 2)
            for odd, lo in ((1, 0), (0, C)):
                o = ps[lo:lo + C, O_BANK, 0:T // 2]
                pe.matmul(o, wcs("proj_out", 0, C), yg[:, odd:T:2], start=True, stop=False)
                mm = pe.matmul(o, wcs("residual", s, C), xn[:, 3 + k * T + odd:3 + k * T + T:2], start=False, stop=True)
            mm.then_inc(S["out_mm"], 1)

        def evacuate(a, tile, par, n_before):
            a.wait_ge(S["out_mm"], tile + 2)
            a.wait_ge(S[f"out_stored{par}"], n_before * 16)
            for half, slot in ((0, 1), (1, 0)):
                src = ps[C * half:C * half + C, O_BANK, 0:T // 2].rearrange("p (r j) -> p r j", j=HALF)
                a.copy(otile[C * half:C * half + C, par, :, slot:slot + HALF], src).then_inc(S["out_evac"], 1)

        def store(sp, tile, par, img, k):
            sp.wait_ge(S["out_evac"], tile * 2 + 4)
            sp.dma_start(x3[img, :, k * TR:(k + 1) * TR, :], otile[:, par, :, :]).then_inc(S[f"out_stored{par}"], 16)

        def ended(p, t):
            tile = p * ST + (t - 1)
            tt = (t - 1) % ST
            par = tt % 2
            before = p * KT + (t // 2 if par else (t - 1) // 2)
            img = (p * 2 + (N - 1)) % N if t == 0 else p * 2 + tt // KT
            return tile, UB[tt], tt // KT, tt % KT, par, before, img

        PE_AT = {0: ["u"], 1: ["z"], 2: ["dt"], 3: ["bc0"], 4: ["bc1"], 5: ["lnc"], 6: ["bc2"], 7: ["lnv"],
                 8: ["bc3"], 9: ["bc4"], 10: ["bc5"], 11: ["bc6"], 12: ["bc7"]}

        COPIES = 1 + 55 + 28 + 1 + 110

        def steps_of(direction):
            return {0: (1, 55), 1: (56, 110), 2: (112, 166), 3: (167, 221)}[direction]

        def scan_loops(e, body, columns_start=lambda: None):
            for d in range(4):
                lo, hi = steps_of(d)
                m = lo
                if d == 2:
                    columns_start()
                while m % 4:
                    body(d, m, m, m // 2)
                    m += 1
                n = (hi + 1 - m) // 4
                with e.Fori(0, n) as i:
                    for r in range(4):
                        body(d, i * 4 + (m + r), m + r, i * 2 + (m + r) // 2)
                m += 4 * n
                while m <= hi:
                    body(d, m, m, m // 2)
                    m += 1

        def position(d, m):
            return {0: m, 1: 110 - m, 2: m - 111, 3: 221 - m}[d] if isinstance(m, int) else \
                (m if d == 0 else 110 - m if d == 1 else m - 111 if d == 2 else 221 - m)

        def mms_before(d, m):
            return m - 1 if d < 2 else m - 2

        block = ctx.enter_context(nc.Block())

        @block.sync
        def _(sp):
            sp.dma_start(wa[:, :], pack_a).then_inc(pack_in, 16)
            sp.wait_ge(pads_zeroed, 1)

            def load_x(i, b):
                im = i * 2 + b
                rows = x[im].rearrange("c (r two) w -> c r two w", two=2)
                sp.dma_start(xpad[0:C, b, 1:HALF + 1, 1:W + 1], rows[:, :, 1, :]).then_inc(sa[f"in_loaded{b}"], 16)
                sp.dma_start(xpad[C:P, b, 0:HALF, 1:W + 1], rows[:, :, 0, :]).then_inc(sa[f"in_loaded{b}"], 16)

            load_x(0, 0)
            load_x(0, 1)
            with sp.Fori(0, PAIRS - 1) as i:
                for b in range(2):
                    sp.wait_ge(sa["conv_done"], i * 8 + (b + 1) * QT)
                    load_x(i + 1, b)
            barrier(sp, 1)
            sp.dma_start(yin[:, 0, :], y1[0]).then_inc(sbm["in_loaded0"], 16)
            sp.dma_start(yin[:, 1, :], y1[1]).then_inc(sbm["in_loaded1"], 16)
            with sp.Fori(0, PAIRS - 1) as i:
                for b in range(2):
                    sp.wait_ge(sbm["padded"], i * 4 + (b + 1) * 2)
                    sp.dma_start(yin[:, b, :], y1[i * 2 + (2 + b)]).then_inc(sbm[f"in_loaded{b}"], 16)
            barrier(sp, 2)
            sp.dma_start(wc[:, :], pack_c).then_inc(pack_in, 16)
            for k in range(6):
                ln_load(sp, Ahead(k))
            st = Ahead()
            stack_parts(sp, st, 0)
            stack_parts(sp, st, 1)
            with sp.Fori(0, PAIRS) as p:
                for t in range(ST):
                    st = Step(p, t)
                    tile, ub, s, k, par, before, img = ended(p, t)
                    if st.has_ln:
                        ln_load(sp, st)
                    stack_parts(sp, st, 0)
                    stack_parts(sp, st, 1)
                    store(sp, tile, par, img, k)
            tile, ub, s, k, par, before, img = ended(PAIRS, 0)
            store(sp, tile, par, N - 1, k)
            sp.wait_ge(S["out_stored1"], (before + 1) * 16)
            sp.wait_ge(S["out_stored0"], before * 16)
            barrier(sp, 3)
            sp.dma_start(wd[:, :], pack_d).then_inc(pack_in, 16)
            sp.dma_start(ws[:, :], pack_s).then_inc(pack_in, 16)
            sp.wait_ge(D["zeroed"], 1)
            with sp.Fori(0, N // 2) as i:
                for b in range(2):
                    sp.wait_ge(D["conv_done"], i * 8 + b * QT + 4)
                    sp.dma_start(xpad3[:, b, 1:H + 1, :], x3[i * 2 + b]).then_inc(D[f"loaded{b}"], 16)

        @block.tensor
        def _(pe):
            conv_pe(pe, sa, 0, (sa["in_loaded0"], sa["in_loaded1"]), 32)
            halves_pe(pe, sa)
            barrier(pe, 1)
            pe.wait_ge(sbm["weights_ready"], 1)
            with pe.Fori(0, PAIRS) as i:
                for b in range(2):
                    pe.wait_ge(sbm["padded"], i * 4 + (b + 1) * 2)
                    for q in range(QT):
                        pe.wait_ge(sbm["psum_free"], i * 8 + b * QT + q + 1)
                        for kx in range(3):
                            for ab in range(2):
                                mm = pe.matmul(ps[:, b * QT + q, 0:QN], signs[:, 1, kx * 2 + ab, :],
                                               xpad[:, b, q * QR + ab:q * QR + ab + QR, kx:kx + W],
                                               start=(kx + ab == 0), stop=(kx + ab == 3))
                        mm.then_inc(sbm["conv_done"], 1)
            halves_pe(pe, sbm)
            barrier(pe, 2)
            pe.wait_ge(pack_in, 32)
            pe.matmul(ps[:, 0, 0:P], wcs("dt_rows", 0, P)[0:HC, :], wcs("dt_rows", 1, P)[0:HC, :],
                      start=True, stop=True).then_inc(S["wdt_mm"], 1)
            pe.wait_ge(S["ready"], 4)
            for k in range(6):
                st = Ahead(k)
                pe_task(pe, st, "lnc")
                pe_task(pe, st, "lnv")
            st = Ahead()
            for name in TASKS:
                if not name.startswith("ln"):
                    pe_task(pe, st, name)
            sum_states(pe, -1, 0)
            sum_states(pe, -1, 1)
            with pe.Fori(0, PAIRS) as p:
                for t in range(ST):
                    st = Step(p, t)
                    tile, ub, s, k, par, before, img = ended(p, t)
                    for j in range(UN):
                        spread(pe, st, j)
                        for name in PE_AT.get(j, ()):
                            if st.has_ln or not name.startswith("ln"):
                                pe_task(pe, st, name)
                        if j == 0:
                            sum_states(pe, tile, 2)
                        if j == 4:
                            sum_states(pe, tile, 3)
                        if j == 8:
                            sum_states(pe, st.tile, 0)
                        if j == 12:
                            sum_states(pe, st.tile, 1)
                        if j == 9:
                            project_out(pe, tile, s, k)
            tile, ub, s, k, par, before, img = ended(PAIRS, 0)
            sum_states(pe, tile, 2)
            sum_states(pe, tile, 3)
            project_out(pe, tile, s, k)
            barrier(pe, 3)
            pe.wait_ge(pack_in, 64)
            a = cd["w2"][0]
            for tap in range(9):
                mm = pe.matmul(ps[:, tap // 5, (tap % 5) * (C + 1):(tap % 5 + 1) * (C + 1)],
                               wd[:, a + tap * P:a + (tap + 1) * P], wd[:, cd["w1b1"][0]:cd["w1b1"][1]],
                               start=True, stop=True)
            mm.then_inc(D["prep_mm"], 1)
            pe.wait_ge(D["prep_v"], 2)
            w3 = wd[:, cd["w3"][0]:cd["w3"][1]]
            for tap in range(9):
                for half in range(2):
                    pe.matmul(ps[C * half:C * half + C, 2 + tap // 5, (tap % 5) * C:(tap % 5 + 1) * C],
                              rmix[:, tap, 0:C], w3, start=True, stop=True)
            for half in range(2):
                o = slice(C * half, C * half + C)
                pe.matmul(ps[o, 4, 0:9], w3, rmix[:, :, C:C + 1].rearrange("p a b -> p (a b)"), start=True, stop=True)
                pe.matmul(ps[o, 5, 0:1], w3, wd[:, cd["b2"][0]:cd["b2"][1]], start=True, stop=False)
                mm = pe.matmul(ps[o, 5, 0:1], wd[:, cd["b3"][0]:cd["b3"][1]], wd[:, cd["ones"][0]:cd["ones"][1]],
                               start=False, stop=True)
            mm.then_inc(D["prep_mm"], 1)
            pe.wait_ge(D["bias_ready"], 1)
            with pe.Fori(0, 2) as g:
                for ch in range(2):
                    pe.wait_ge(D[f"row{ch}"], g * 220)
                pe.sem_inc(D["gates"], 1)
                with pe.Fori(0, GRP // 2) as i:
                    for b in range(2):
                        pe.wait_ge(D[f"loaded{b}"], (g * (GRP // 2) + i) * 16 + 16)
                        for q in range(QT):
                            pe.wait_ge(D["evacuated"], (g * (GRP // 2) + i) * 8 + b * QT + q + 1)
                            for ky in range(3):
                                for ab in range(2):
                                    mm = pe.matmul(ps[:, b * QT + q, 0:QN], lw[:, ky * 2 + ab, :],
                                                   xpad3[:, b, q * (H // QT) + ky:(q + 1) * (H // QT) + ky, ab:ab + HALF],
                                                   start=(ky + ab == 0), stop=(ky + ab == 3))
                            mm.then_inc(D["conv_done"], 1)

                def body(d, m, mi, half):
                    for ch in range(2):
                        if mi == 1:
                            pe.wait_ge(D[f"copied{ch}"], g * COPIES + 1)
                        else:
                            pe.wait_ge(D[f"row{ch}"], g * 220 + mms_before(d, m))
                        for s in range(KS):
                            w0 = (d * KS + s) * P
                            mm = pe.matmul(ps[:, 2 * ch + mi % 2, 0:CH * HALF], ws[:, w0:w0 + P],
                                           pv[:, ch, (mi - 1) % 4, :, s:s + HALF], start=(s == 0), stop=(s == KS - 1))
                        mm.then_inc(D[f"mm{ch}"], 1)

                def columns_start():
                    for ch in range(2):
                        pe.wait_ge(D[f"copied{ch}"], g * COPIES + 85)
                    pe.sem_inc(D["gates"], 1)
                scan_loops(pe, body, columns_start)

        @block.scalar
        def _(a):
            a.wait_ge(pack_in, 16)
            a.activation(signs[:, 0, :, :], wa[:, ca["conv1"][0]:ca["conv1"][1]].rearrange("p (t m) -> p t m", m=P),
                         ACT.Sign).then_inc(sa["weights_ready"], 1)
            a.activation(signs[:, 1, :, :], wa[:, ca["conv2"][0]:ca["conv2"][1]].rearrange("p (t m) -> p t m", m=P),
                         ACT.Sign).then_inc(sbm["weights_ready"], 1)
            with a.Fori(0, PAIRS) as i:
                for b in range(2):
                    a.wait_ge(sa["out_ready"], i * 8 + (b + 1) * QT)
                    a.dma_start(y1[i * 2 + b], yout[:, b, :]).then_inc(sa[f"stored{b}"], 16)
            for b in range(2):
                a.wait_ge(sa[f"stored{b}"], 16 * PAIRS)
            rstd_act(a, sa)
            barrier(a, 1)
            def norm(i, b, first):
                a.wait_ge(sbm[f"in_loaded{b}"], (i + 1) * 16)
                if not first:
                    a.wait_ge(sbm["conv_done"], i * 8 + b * QT - 4)
                for half, slot in ((0, 1), (1, 0)):
                    o = slice(C * half, C * half + C)
                    a.activation(xpad[o, b, slot:slot + HALF, 1:W + 1],
                                 yin[o, b, :].rearrange("p (r w) -> p r w", w=W), ACT.Relu,
                                 bias=bn[o, SHIFT1:SHIFT1 + 1], scale=bn[o, SCALE1:SCALE1 + 1]).then_inc(sbm["padded"], 1)

            def put(i, b):
                a.wait_ge(sbm["out_ready"], i * 8 + (b + 1) * QT)
                rows = y2[i * 2 + b].rearrange("c (r two) w -> c r two w", two=2)
                for half, odd in ((0, 1), (1, 0)):
                    a.dma_start(rows[:, :, odd, :], yout[C * half:C * half + C, b, :].rearrange("p (r w) -> p r w", w=W))\
                        .then_inc(sbm[f"stored{b}"], 16)
            norm(0, 0, True)
            norm(0, 1, True)
            with a.Fori(0, PAIRS - 1) as i:
                for b in range(2):
                    norm(i + 1, b, False)
                    put(i, b)
            put(PAIRS - 1, 0)
            put(PAIRS - 1, 1)
            for b in range(2):
                a.wait_ge(sbm[f"stored{b}"], 32 * PAIRS)
            rstd_act(a, sbm)
            barrier(a, 2)
            a.wait_ge(pack_in, 32)
            a.preload_act_table_set("natural_log_exp_and_others")
            a.activation(nega[:, :], wcs("a_log", 0, 4), ACT.Exp).then_inc(S["prep"], 1)
            a.wait_ge(S["prep"], 1)
            a.activation(nega[:, :], nega[:, :], ACT.Copy, scale=-1.0).then_inc(S["ready"], 1)
            a.wait_ge(S["ready"], 4)
            for k in range(6):
                st = Ahead(k)
                ln_relu(a, st)
                act_task(a, st, "lnc")
                act_task(a, st, "lnv")
                ln_shift(a, st)
            st = Ahead()
            for name in TASKS:
                if name == "u":
                    a.preload_act_table_set("silu_and_others")
                if name == "dt":
                    a.preload_act_table_set("natural_log_exp_and_others")
                if not name.startswith("ln"):
                    act_task(a, st, name)
            with a.Fori(0, PAIRS) as p:
                for t in range(ST):
                    st = Step(p, t)
                    tile, ub, s, k, par, before, img = ended(p, t)
                    for j in range(UN):
                        decay(a, st, j)
                        if j == 4 and st.has_ln:
                            ln_relu(a, st)
                        for name in PE_AT.get(j, ()):
                            if name in ("u", "z"):
                                continue
                            if name == "dt":
                                a.preload_act_table_set("silu_and_others")
                                act_task(a, st, "u")
                                act_task(a, st, "z")
                                a.preload_act_table_set("natural_log_exp_and_others")
                            if st.has_ln or not name.startswith("ln"):
                                act_task(a, st, name)
                        if j == 10:
                            evacuate(a, tile, par, before)
                        if j == 12 and st.has_ln:
                            ln_shift(a, st)
            tile, ub, s, k, par, before, img = ended(PAIRS, 0)
            evacuate(a, tile, par, before)
            barrier(a, 3)
            with a.Fori(0, 2) as g:
                for ch in range(2):
                    a.wait_ge(D["evacuated"], (g + 1) * GRP * QT + 8)
                    a.copy(pv[:, ch, 0, :, PADS:PADS + HALF], R[:, ch * CH:(ch + 1) * CH, 0:HALF])\
                        .then_inc(D[f"copied{ch}"], 1)

                def body(d, m, mi, half):
                    r = position(d, m)
                    for ch in range(2):
                        im = slice(ch * CH, (ch + 1) * CH)
                        new = pv[:, ch, mi % 4, :, PADS:PADS + HALF]
                        if d == 0:
                            a.wait_ge(D[f"row{ch}"], g * 220 + m)
                            a.copy(R[:, im, bass.ds(r * HALF, HALF)], new).then_inc(D[f"copied{ch}"], 1)
                        elif d == 1:
                            if mi % 2:
                                continue
                            a.wait_ge(D[f"row{ch}"], g * 220 + m)
                            a.wait_ge(D[f"copied{ch}"], g * COPIES + 28 + half)
                            for odd in range(2):
                                for wp in range(2):
                                    o = slice(0, C) if odd else slice(C, P)
                                    i_ = slice(0, C) if wp else slice(C, P)
                                    dst = R[o, im, bass.ds(r * HALF, 2 * HALF)].rearrange("p n (j two) -> p n j two", two=2)
                                    ins = a.copy(dst[:, :, :, wp],
                                                 pv[i_, ch, (mi - odd) % 4, :, PADS:PADS + HALF])
                            ins.then_inc(D[f"copied{ch}"], 1)
                        else:
                            a.wait_ge(D[f"row{ch}"], g * 220 + mms_before(d, m) + 1)
                            a.wait_ge(D[f"copied{ch}"], g * COPIES + (m - 28 if d == 3 else 85))
                            dst = R[:, im, :].rearrange("p n (j w) -> p n j w", w=W)
                            a.copy(dst[:, :, :, bass.ds(r, 1)].rearrange("p n j w -> p n (j w)"), new)\
                                .then_inc(D[f"copied{ch}"], 1)
                        if mi == 110:
                            a.wait_ge(D[f"copied{ch}"], g * COPIES + 56 + 28)
                            src = R[:, im, :].rearrange("p n (j w) -> p n j w", w=W)
                            a.copy(pv[:, ch, 3, :, PADS:PADS + HALF], src[:, :, :, 0]).then_inc(D[f"copied{ch}"], 1)
                scan_loops(a, body)
                for ch in range(2):
                    a.wait_ge(D[f"copied{ch}"], (g + 1) * COPIES)
                with a.Fori(0, GRP) as n:
                    for half in range(2):
                        rows = out[g * GRP + n].rearrange("c (r two) w -> c r two w", two=2)
                        a.dma_start(rows[:, :, 1 - half, :],
                                    R[C * half:C * half + C, n, :].rearrange("p (r w) -> p r w", w=W))\
                            .then_inc(D["stored"], 16)
                a.wait_ge(D["stored"], (g + 1) * GRP * 32)

        @block.vector
        def _(v):
            v.memset(xpad[:, :, :, :], 0.0).then_inc(pads_zeroed, 1)
            v.sem_inc(sa["psum_free"], 8)
            v.sem_inc(sbm["psum_free"], 8)
            with v.Fori(0, PAIRS) as i:
                for b in range(2):
                    conv_dve(v, sa, i, b)
            batch_stats(v, sa, 0, SCALE1, SHIFT1)
            barrier(v, 1)
            with v.Fori(0, PAIRS) as i:
                for b in range(2):
                    conv_dve(v, sbm, i, b)
            batch_stats(v, sbm, 2, SCALE2, SHIFT2)
            barrier(v, 2)
            v.memset(xn[:, :], 0.0)
            v.memset(u[:, 3, :], 0.0)
            v.memset(otile[:, :, :, :], 0.0)
            v.memset(hs[:, :, :], 0.0).then_inc(S["ready"], 1)
            v.wait_ge(pack_in, 32)
            for s in range(2):
                for k in range(4):
                    ins = v.tensor_tensor(wtap[:, s, k, :], wcs("conv_in", s, P), wcs("taps", k, P), ALU.mult)
            v.tensor_copy(seld[:, :, :], wc[:, cc["select_d"][0]:cc["select_d"][1]].rearrange("p (b m) -> p b m", m=P))
            v.wait_ge(S["wdt_mm"], 1)
            v.tensor_copy(wdt[:, :], ps[:, 0, 0:P]).then_inc(S["ready"], 1)
            v.wait_ge(S["ready"], 4)
            v.sem_inc(S["exp_done"], 2)
            v.sem_inc(S["dbu_done"], 2)
            v.sem_inc(S["scan_done"], 4)
            v.sem_inc(S["prod_done"], 16)
            for k in range(6):
                st = Ahead(k)
                ln_sum(v, st)
                ln_scale(v, st)
            st = Ahead()
            delta_q(v, st)
            delta_sum(v, st)
            split(v, st, 0)
            split(v, st, 1)
            with v.Fori(0, PAIRS) as p:
                for t in range(ST):
                    st = Step(p, t)
                    tile, ub, s, k, par, before, img = ended(p, t)
                    drive(v, st, 0)
                    for j in range(UN):
                        if j + 1 < UN:
                            drive(v, st, j + 1)
                        scan(v, st, j)
                        if j == 3 and st.has_ln:
                            ln_sum(v, st)
                        if j == 4:
                            delta_q(v, st)
                        if j == 5:
                            add_du(v, tile, ub)
                        if j == 6:
                            delta_sum(v, st)
                            split(v, st, 0)
                        if j == 9:
                            split(v, st, 1)
                        if j == 10 and st.has_ln:
                            ln_scale(v, st)
            tile, ub, s, k, par, before, img = ended(PAIRS, 0)
            add_du(v, tile, ub)
            barrier(v, 3)
            v.memset(xpad3[:, :, :, :], 0.0).then_inc(D["zeroed"], 1)
            v.sem_inc(D["conv_done"], 8)
            v.memset(pv[:, :, :, :, :], 0.0)
            v.memset(lw[:, :, :], 0.0)
            v.wait_ge(D["prep_mm"], 1)
            n = [0]

            def step(ins):
                n[0] += 1
                ins.then_inc(D["prep_v"], 1)
                v.wait_ge(D["prep_v"], n[0])
            step(v.tensor_copy(rmix[:, 0:5, :], ps[:, 0, 0:5 * (C + 1)].rearrange("p (t c) -> p t c", c=C + 1)))
            step(v.tensor_copy(rmix[:, 5:9, :], ps[:, 1, 0:4 * (C + 1)].rearrange("p (t c) -> p t c", c=C + 1)))
            v.wait_ge(D["prep_mm"], 2)
            lo, hi = slice(0, C), slice(C, P)

            def tap(part, ky, kx):
                i = ky * 3 + kx
                return ps[part, 2 + i // 5, (i % 5) * C:(i % 5 + 1) * C]
            ident = wd[:, cd["ident"][0]:cd["ident"][1]]
            for ky in range(3):
                for ab, kin, kout, kx in ((0, lo, hi, 0), (0, hi, lo, 0), (0, hi, hi, 1),
                                          (1, lo, lo, 1), (1, lo, hi, 2), (1, hi, lo, 2)):
                    dst = lw[kin, ky * 2 + ab, kout]
                    if (ky, kx) == (1, 1):
                        ins = v.tensor_tensor(dst, tap(kin, ky, kx), ident[kin, :], ALU.add)
                    else:
                        ins = v.tensor_copy(dst, tap(kin, ky, kx))
            step(ins)
            step(v.tensor_copy(bt[:, 0:9], ps[:, 4, 0:9]))
            step(v.tensor_copy(bt[:, 9:10], ps[:, 5, 0:1]))
            step(v.tensor_reduce(bt[:, 10:11], bt[:, 0:10], mybir.AxisListType.X, ALU.add))
            step(v.memset(bmap[:, :, :], 0.0))
            step(v.tensor_scalar(bmap[:, :, :], bmap[:, :, :], bt[:, 10:11], None, ALU.add))

            def drop(part, rows, cols, taps, op):
                for i in taps:
                    ap = bmap[part, rows, cols]
                    step(v.tensor_scalar(ap, ap, bt[part, i:i + 1], None, op))
            every = slice(0, P)
            drop(every, slice(0, 1), slice(0, HALF), (0, 1, 2), ALU.subtract)
            drop(every, slice(H - 1, H), slice(0, HALF), (6, 7, 8), ALU.subtract)
            drop(hi, slice(0, H), slice(0, 1), (0, 3, 6), ALU.subtract)
            drop(lo, slice(0, H), slice(HALF - 1, HALF), (2, 5, 8), ALU.subtract)
            for part, cl, r, i in ((hi, 0, 0, 0), (lo, HALF - 1, 0, 2), (hi, 0, H - 1, 6), (lo, HALF - 1, H - 1, 8)):
                drop(part, slice(r, r + 1), slice(cl, cl + 1), (i,), ALU.add)
            v.sem_inc(D["evacuated"], 8)
            v.sem_inc(D["bias_ready"], 1)
            bm = bmap[:, :, :].rearrange("p h j -> p (h j)")
            with v.Fori(0, 2) as g:
                v.wait_ge(D["stored"], g * GRP * 32)
                v.sem_inc(D["gates"], 1)
                with v.Fori(0, GRP // 2) as i:
                    for b in range(2):
                        for q in range(QT):
                            v.wait_ge(D["conv_done"], (g * (GRP // 2) + i) * 8 + b * QT + q + 1 + 8)
                            v.tensor_tensor(R[:, i * 2 + b, q * QN:(q + 1) * QN], ps[:, b * QT + q, 0:QN],
                                            bm[:, q * QN:(q + 1) * QN], ALU.add).then_inc(D["evacuated"], 1)
                v.wait_ge(D["evacuated"], (g + 1) * GRP * QT + 8)

                def copied_by(d, m, mi, half):
                    if d == 0:
                        return m - 3
                    if d == 1:
                        return half + 27 + mi % 2
                    if mi == 167:
                        return 139
                    return m - 30

                def body(d, m, mi, half):
                    r = position(d, m)
                    for ch in range(2):
                        im = slice(ch * CH, (ch + 1) * CH)
                        v.wait_ge(D[f"mm{ch}"], g * 220 + mms_before(d, m) + 1)
                        if mi >= 4:
                            v.wait_ge(D[f"copied{ch}"], g * COPIES + copied_by(d, m, mi, half))
                        if d < 2:
                            cur = R[:, im, bass.ds(r * HALF, HALF)]
                        else:
                            cur = R[:, im, :].rearrange("p n (j w) -> p n j w", w=W)[:, :, :, bass.ds(r, 1)]\
                                .rearrange("p n j w -> p n (j w)")
                        v.scalar_tensor_tensor(pv[:, ch, mi % 4, :, PADS:PADS + HALF],
                                               ps[:, 2 * ch + mi % 2, 0:CH * HALF].rearrange("p (n j) -> p n j", j=HALF),
                                               0.0, cur, ALU.max, ALU.add).then_inc(D[f"row{ch}"], 1)

                def columns_start():
                    for ch in range(2):
                        v.wait_ge(D[f"copied{ch}"], g * COPIES + 85)
                    v.sem_inc(D["gates"], 1)
                scan_loops(v, body, columns_start)

        @block.gpsimd
        def _(g):
            barrier(g, 1)
            barrier(g, 2)
            g.memset(prod[:, :, :], 0.0)
            g.memset(sz[:, 3, :], 0.0).then_inc(S["ready"], 1)
            g.wait_ge(S["ready"], 4)
            st = Ahead()
            delta_s(g, st)
            delta_times_u(g, st)
            with g.Fori(0, PAIRS) as p:
                for t in range(ST):
                    st = Step(p, t)
                    tile, ub, s, k, par, before, img = ended(p, t)
                    for j in range(UN):
                        times_c(g, st, j)
                        if j == 4:
                            delta_s(g, st)
                        if j == 5:
                            gate(g, tile, ub)
                        if j == 7:
                            delta_times_u(g, st)
            tile, ub, s, k, par, before, img = ended(PAIRS, 0)
            gate(g, tile, ub)
            barrier(g, 3)


def pack(np, parts, layout):
    cols, n = columns(layout)
    out = np.zeros((P, n), np.float32)
    for name, a in parts.items():
        lo, hi = cols[name]
        out[:a.shape[0], lo:hi] = a.reshape(a.shape[0], hi - lo)
    return out


def pair_blocks(np, w, rows):
    o = np.zeros((2, C, 3, 2, 2, C), np.float32)
    for ab, kin, kout, ky in ((0, 0, 1, 0), (0, 1, 0, 0), (0, 1, 1, 1), (1, 0, 0, 1), (1, 0, 1, 2), (1, 1, 0, 2)):
        for kx in range(3):
            o[kin, :, kx, ab, kout, :] = w[ky, kx]
    return o.reshape(P, 6 * P)


def scan_blocks(np, k):
    o = np.zeros((2, C, KS, 2, C), np.float32)
    for s in range(KS):
        for kin in range(2):
            for kout in range(2):
                tap = 2 * (s - 2) + (1 - kin) - (1 - kout) + 4
                if 0 <= tap < KW:
                    o[kin, :, s, kout, :] = k[tap]
    return o.reshape(P, KS * P)


def lay_out(np, a):
    eye = np.eye(C, dtype=np.float32)
    two = lambda v: np.concatenate([v, v])[:, None]
    c1, c2 = a["L0_conv_w1"].transpose(2, 3, 1, 0), a["L0_conv_w2"].transpose(2, 3, 1, 0)
    pa = pack(np, {
        "conv1": pair_blocks(np, c1, 0), "conv2": pair_blocks(np, c2, 0),
        "halves": np.tile(eye / 2, (2, 2)),
        "vecs": np.concatenate([two(a[f"L0_conv_{n}"]) for n in ("gamma1", "beta1", "gamma2", "beta2")]
                               + [np.full((P, 1), EPS, np.float32)], 1)}, PACK_A)
    ip = a["L1_conv_in_proj_w"]
    cm = C // HC
    conv_in, gate_in = (np.zeros((2, HC, cm, 2, HC, DI), np.float32) for _ in range(2))
    out_w = np.zeros((HC, DI, HC, cm), np.float32)
    bc = np.zeros((HC, DI, HC, 2, 8, NS), np.float32)
    dtr = np.zeros((HC, 2, HC, DI), np.float32)
    xp = a["L1_conv_x_proj_w"]
    for c in range(HC):
        for s in range(2):
            conv_in[s, c, :, s, c, :] = ip[:DI].T
            gate_in[s, c, :, s, c, :] = ip[DI:].T
        out_w[c, :, c, :] = a["L1_conv_out_proj_w"].T
        for i in range(2):
            bc[c, :, c, i] = xp[1 + NS * i:1 + NS * (i + 1)].T[:, None, :]
        dtr[c, 0, c] = xp[0]
        dtr[c, 1, c] = a["L1_conv_dt_proj_w"][:, 0]
    four = lambda v: np.tile(v, HC)[:, None]
    d_of = np.arange(P) // NS
    sel_d = np.zeros((P, 4, P), np.float32)
    red = np.zeros((P, 4, DI), np.float32)
    for b in range(4):
        for part in range(3):
            sel_d[32 * part + 8 * b + d_of, b, np.arange(P)] = 1
        red[np.arange(P), b, 8 * b + d_of] = 1
    block = np.zeros((2, C, 2, C), np.float32)
    for s in range(2):
        block[s, :, s] = 1 / C
    mean = block.reshape(P, P)
    res = np.zeros((2, C, 2, C), np.float32)
    for s in range(2):
        res[s, :, s] = eye
    pc = pack(np, {
        "conv_in": conv_in.reshape(P, 2 * P), "gate_in": gate_in.reshape(P, 2 * P),
        "taps": np.broadcast_to(np.tile(a["L1_conv_conv_w"].T, (1, HC)).reshape(1, 4 * P), (P, 4 * P)),
        "spread_bc": bc.reshape(P, 2 * HC * P), "select_d": sel_d, "reduce_n": red,
        "proj_out": out_w.reshape(P, C), "residual": res.reshape(P, 2 * C),
        "centre": np.eye(P, dtype=np.float32) - mean, "average": mean, "dt_rows": dtr.reshape(HC, 2 * P),
        "vecs": np.concatenate([two(a["L1_conv_ln_g"]), two(a["L1_conv_ln_b"]), four(a["L1_conv_conv_b"]),
                                four(a["L1_conv_dt_proj_b"]), four(a["L1_conv_D"]),
                                np.full((P, 1), EPS, np.float32)], 1),
        "a_log": a["L1_conv_A_log"].reshape(4, P).T}, PACK_C)
    w2 = np.zeros((32, 4, 9, 32, 4), np.float32)
    for g in range(32):
        w2[g, :, :, g, :] = a["L2_conv_W2"][g].transpose(1, 2, 3, 0).reshape(4, 9, 4)
    pd = pack(np, {
        "w1b1": np.concatenate([a["L2_conv_W1"].reshape(P, C), a["L2_conv_b1"].reshape(P, 1)], 1),
        "w2": w2.reshape(P, 9 * P), "w3": a["L2_conv_W3"].transpose(0, 2, 1).reshape(P, C),
        "ident": np.tile(eye, (2, 1)), "b3": a["L2_conv_b3"], "ones": np.ones((P, 1), np.float32),
        "b2": a["L2_conv_b2"].reshape(P, 1)}, PACK_D)
    psc = pack(np, {"scan": np.concatenate([scan_blocks(np, a[f"L3_conv_k_{n}"]) for n in ("td", "dt", "lr", "rl")], 1)},
               PACK_S)
    return {"x": np.ascontiguousarray(a["x"]), "pack_a": pa, "pack_c": pc, "pack_d": pd, "pack_s": psc}


def kernel(**inputs):
    import numpy as _np
    import concourse.bacc as _bacc
    from concourse import mybir as _mybir
    from concourse.bass_utils import run_bass_kernel_spmd as _run

    nc = _bacc.Bacc("TRN2", target_bir_lowering=False, num_devices=1)
    arrays = lay_out(_np, {k: _np.asarray(v) for k, v in inputs.items()})
    aps = [nc.dram_tensor(f"in_{n}", v.shape, _mybir.dt.float32, kind="ExternalInput").ap() for n, v in arrays.items()]
    out = nc.dram_tensor("out_0", arrays["x"].shape, _mybir.dt.float32, kind="ExternalOutput").ap()
    build(nc, *aps, out)
    r = _run(nc, [{f"in_{n}": v for n, v in arrays.items()}], core_ids=[0])
    return r.results[0]["out_0"]
```

```python
from contextlib import ExitStack

import concourse.bass as bass
from concourse import mybir

ALU = mybir.AluOpType
ACT = mybir.ActivationFunctionType
F32 = mybir.dt.float32
BF16 = mybir.dt.bfloat16
F32R = mybir.dt.float32r

P = 128
C = 64
HC = 4
GR = 4
DI = 32
NS = 16
H = W = 56
HW = H * W
HALF = W // 2
PIX = H * HALF
KW = 9
KS = 5
PADS = 2
EPS = 1e-5

PE_AT = {0: ["bc0", "last3"], 3: ["bc1"], 5: ["lnc"], 7: ["sum0"], 8: ["project", "lnv"], 10: ["tap0", "tap2"],
         12: ["tap1"], 13: ["tap3", "sum1", "z", "dt"], 14: ["sum2"]}
ACT_AT = {1: ["bc0"], 2: ["relu"], 4: ["bc1"], 5: ["cast0"], 7: ["cast1"], 8: ["lnc"], 11: ["lnv"],
          12: ["shift", "evacuate"], 14: ["silu", "u", "z", "exp"], 15: ["dt"]}
DVE_AT = {0: ["add_x"], 3: ["min", "gate"], 6: ["rest0"], 8: ["rest1"], 10: ["scale"]}
POOL_AT = {0: ["delta_log", "delta", "delta_u"]}
LEAD = {"du": 2, "delta": 3, "decay": 2, "drive": 1}
TASKS = [{"tap0": "u"}.get(n, n) for j in range(16) for n in PE_AT.get(j, ())
         if n[:2] in ("bc", "ln", "z", "dt") or n == "tap0"]

PACK_A = [("conv1", 6 * P), ("conv2", 6 * P), ("halves", P), ("vecs", 5)]
PACK_C = [("conv_in", 2 * P), ("gate_in", 2 * P), ("taps", 4 * P), ("spread_bc", 2 * P),
          ("select_d", 4 * P), ("reduce_n", 4 * DI), ("skip", P), ("proj_out", C), ("residual", 2 * C),
          ("centre", P), ("average", P), ("dt_rows", 2 * P), ("vecs", 6), ("a_log", 16)]
PACK_D = [("w1b1", C + 1), ("w2", 9 * P), ("w3", C), ("ident", C), ("b3", C), ("ones", 1), ("b2", 1)]
PACK_S = [("scan", 4 * KS * P)]


def columns(pack):
    at, out = 0, {}
    for name, n in pack:
        out[name] = (at, at + n)
        at += n
    return out, at


def build(nc, x, pack_a, pack_c, pack_d, pack_s, out):
    N = x.shape[0]
    PAIRS = N // 2
    QT = 4
    QR = HALF // QT
    QN = QR * W
    T = 448
    TR = T // W
    KT = HW // T
    ST = 2 * KT
    UN = 4 * GR
    GRP = N // 2
    CH = GRP // 2
    assert CH % 2 == 0

    ca, na = columns(PACK_A)
    cc, ncc = columns(PACK_C)
    cd, nd = columns(PACK_D)
    cs, ns = columns(PACK_S)

    y1 = nc.dram_tensor("y1_pairs", (N, P, PIX), F32, kind="Internal").ap()
    y2 = nc.dram_tensor("y2_nchw", (N, C, H, W), F32, kind="Internal").ap()
    x3 = nc.dram_tensor("x3_column_pairs", (N, P, H, HALF + 1), F32, kind="Internal").ap()

    with ExitStack() as ctx:
        def sem(name):
            return ctx.enter_context(nc.semaphore(name))

        def sb(stack, name, shape, dt=F32):
            return stack.enter_context(nc.sbuf_tensor(name, shape, dt))

        ps = ctx.enter_context(nc.psum_tensor("ps", [P, 8, 512], F32))
        bn = sb(ctx, "bn", [P, 24])

        with ExitStack() as m:
            wa = sb(m, "wa", [P, na])
            signs = sb(m, "signs", [P, 2, 6, P], F32R)
            xpad = sb(m, "xpad", [P, 2, HALF + 1, W + 2])
            xparts = sb(m, "xparts", [P, 2, 2, HALF + 1, W + 2], F32R)
            yin = sb(m, "yin", [P, 2, PIX])
            yout = sb(m, "yout", [P, 2, PIX])
            stats = sb(m, "stats", [P, N * QT, 6])
        with ExitStack() as m:
            wc = sb(m, "wc", [P, ncc])
            wtap = sb(m, "wtap", [P, 2, 4, P])
            wdt = sb(m, "wdt", [P, P])
            seld = sb(m, "seld", [P, 4, P], BF16)
            nega = sb(m, "nega", [P, UN])
            lnx = sb(m, "lnx", [P, T])
            lny = sb(m, "lny", [P, T])
            xsum = sb(m, "xsum", [P, T])
            xres = sb(m, "xres", [P, T])
            xcen = sb(m, "xcen", [P, T])
            xsq = sb(m, "xsq", [P, T])
            xvar = sb(m, "xvar", [P, T])
            xrstd = sb(m, "xrstd", [P, T])
            xg = sb(m, "xg", [P, T])
            xn = sb(m, "xn", [P, 3 + HW])
            u = sb(m, "u", [P, 4, T])
            sz = sb(m, "sz", [P, 4, T])
            dabs = sb(m, "dabs", [P, T])
            drelu = sb(m, "drelu", [P, T])
            dexp = sb(m, "dexp", [P, T])
            dln = sb(m, "dln", [P, T])
            dw = sb(m, "dw", [P, T])
            dq = sb(m, "dq", [P, T])
            ds1 = sb(m, "ds1", [P, T])
            ds2 = sb(m, "ds2", [P, T])
            dlt = sb(m, "dlt", [P, 2, T])
            rest = sb(m, "rest", [P, 2, T])
            parts = sb(m, "parts", [P, 2, 3, T], BF16)
            stack = sb(m, "stack", [96, 2, 2, GR, T], BF16)
            bsp = sb(m, "bsp", [P, 2, 2, T])
            da = sb(m, "da", [P, 8, T])
            dbu = sb(m, "dbu", [P, 8, T])
            hs = sb(m, "hs", [P, UN, T])
            prod = sb(m, "prod", [P, 8, T])
            yg = sb(m, "yg", [P, T])
            otile = sb(m, "otile", [P, 2, TR, HALF + 1])
        with ExitStack() as m:
            wd = sb(m, "wd", [P, nd])
            ws = sb(m, "ws", [P, ns])
            rmix = sb(m, "rmix", [P, 9, C + 1])
            lw = sb(m, "lw", [P, 6, P])
            bt = sb(m, "bt", [P, 16])
            bmap = sb(m, "bmap", [P, H, HALF])
            xpad3 = sb(m, "xpad3", [P, 2, H + 2, HALF + 1])
            R = sb(m, "R", [P, GRP, PIX])
            pv = sb(m, "pv", [P, 2, 4, CH, HALF + 2 * PADS])

        phase_done = sem("phase_done")
        pack_in = sem("pack_in")

        def barrier(e, k):
            e.drain().then_inc(phase_done, 1)
            e.wait_ge(phase_done, 5 * k)

        def conv_sems(s):
            return {n: sem(f"{s}_{n}") for n in (
                "weights_ready", "in_loaded0", "in_loaded1", "padded", "high", "split",
                "conv_done", "psum_free",
                "stored0", "stored1", "out_ready", "stat_chain", "stat_mean", "stat_halves",
                "stat_var", "stat_rstd")}
        sa, sbm = conv_sems("a"), conv_sems("b")
        pads_zeroed = sem("pads_zeroed")

        S = {n: sem("c_" + n) for n in (
            "gates", "prep", "wdt_mm", "ready", "ln_loaded", "x_summed", "x_relu", "centred",
            "squared", "var_copied", "rstd", "scaled", "xn_ready",
            "tmp_done", "u_ready", "sz_ready", "d_abs", "d_relu", "d_exp", "d_ln", "d_w", "d_q",
            "d_s1", "d_s2", "d_min", "delta", "delta_u",
            "cast", "rest", "split", "stacked",
            "bc_ready", "d_spread", "du_spread", "exp_done", "dbu_done", "scan_done", "prod_done",
            "y_summed", "y_gated", "out_mm", "out_evac", "out_stored0", "out_stored1")}

        D = {n: sem("d_" + n) for n in (
            "loaded0", "loaded1", "zeroed", "gates", "prep_mm", "prep_v", "bias_ready", "conv_done", "evacuated",
            "mm0", "mm1", "row0", "row1", "copied0", "copied1", "stored0", "stored1")}

        def vec_a(i):
            return wa[:, ca["vecs"][0] + i:ca["vecs"][0] + i + 1]

        def vec_c(i):
            return wc[:, cc["vecs"][0] + i:cc["vecs"][0] + i + 1]

        def wcs(name, i, n):
            a = cc[name][0] + i * n
            return wc[:, a:a + n]

        SCALE1, SHIFT1, SCALE2, SHIFT2 = 10, 11, 12, 13

        def col(i, n=1):
            return bn[:, i:i + n]

        def conv_pe(pe, s, layer):
            pe.wait_ge(s["weights_ready"], 1)
            with pe.Fori(0, PAIRS) as i:
                for b in range(2):
                    pe.wait_ge(s["split"], i * 2 + (b + 1))
                    for q in range(QT):
                        pe.wait_ge(s["psum_free"], i * 8 + b * QT + q + 1)
                        for kx in range(3):
                            for ab in range(2):
                                for part in range(2):
                                    mm = pe.matmul(ps[:, b * QT + q, 0:QN], signs[:, layer, kx * 2 + ab, :],
                                                   xparts[:, b, part, q * QR + ab:q * QR + ab + QR, kx:kx + W],
                                                   start=(kx + ab + part == 0), stop=(kx + ab + part == 4))
                        mm.then_inc(s["conv_done"], 1)

        def split_high(v, s, n, b, ready, count):
            v.wait_ge(ready, count)
            if not isinstance(n, int) or n:
                v.wait_ge(s["conv_done"], n * 4)
            v.tensor_copy(xparts[:, b, 0, :, :], xpad[:, b, :, :]).then_inc(s["high"], 1)

        def split_low(v, s, n, b):
            v.wait_ge(s["high"], n + 1)
            v.tensor_tensor(xparts[:, b, 1, :, :], xpad[:, b, :, :], xparts[:, b, 0, :, :].bitcast(F32), ALU.subtract)\
                .then_inc(s["split"], 1)

        def conv_dve(v, s, ready, i, b, last=False):
            n = i * 2 + b
            for q in range(QT):
                if q == 0 and not last:
                    split_high(v, s, n + 1, 1 - b, *ready(i + b, 1 - b))
                if q == 2 and not last:
                    split_low(v, s, n + 1, 1 - b)
                v.wait_ge(s["conv_done"], n * 4 + (q + 5))
                if q == 0:
                    v.wait_ge(s[f"stored{b}"], i * s["store_steps"] + 16)
                v.tensor_copy(yout[:, b, q * QN:(q + 1) * QN], ps[:, b * QT + q, 0:QN]).then_inc(s["out_ready"], 1)
                v.bn_stats(stats[:, i * 8 + (b * QT + q), :], ps[:, b * QT + q, 0:QN]).then_inc(s["psum_free"], 1)

        def convs_dve(v, s, ready):
            split_high(v, s, 0, 0, *ready(0, 0))
            split_low(v, s, 0, 0)
            with v.Fori(0, PAIRS - 1) as i:
                for b in range(2):
                    conv_dve(v, s, ready, i, b)
            conv_dve(v, s, ready, PAIRS - 1, 0)
            conv_dve(v, s, ready, PAIRS - 1, 1, last=True)

        def batch_stats(v, s, g0, scale, shift):
            n = [0]

            def step(ins):
                n[0] += 1
                ins.then_inc(s["stat_chain"], 1)
                v.wait_ge(s["stat_chain"], n[0])

            v.wait_ge(s["psum_free"], 8 * PAIRS + 8)
            step(v.bn_aggr(col(0, 2), stats[:, :, :]))
            step(v.tensor_copy(col(2), col(0)))
            v.scalar_tensor_tensor(col(3), col(0), col(0), col(1), ALU.mult, ALU.add).then_inc(s["stat_mean"], 1)
            v.wait_ge(s["stat_halves"], 1)
            step(v.tensor_copy(col(4, 2), ps[:, 0, 0:2]))
            step(v.tensor_scalar(col(6), col(4), -1.0, None, ALU.mult))
            v.scalar_tensor_tensor(col(7), col(4), col(6), col(5), ALU.mult, ALU.add).then_inc(s["stat_var"], 1)
            v.wait_ge(s["stat_rstd"], 2)
            step(v.tensor_scalar(col(7), col(7), EPS, -0.5, ALU.add, ALU.mult))
            step(v.tensor_tensor(col(9), col(8), col(8), ALU.mult))
            step(v.tensor_scalar(col(9), col(9), col(7), 1.5, ALU.mult, ALU.add))
            step(v.tensor_tensor(col(8), col(8), col(9), ALU.mult))
            step(v.tensor_tensor(col(scale), vec_a(g0), col(8), ALU.mult))
            step(v.scalar_tensor_tensor(col(shift), col(scale), col(6), vec_a(g0 + 1), ALU.mult, ALU.add))

        def rstd_act(a, s):
            a.wait_ge(s["stat_var"], 1)
            a.activation(col(14), col(7), ACT.Ln, bias=vec_a(4)).then_inc(s["stat_rstd"], 1)
            a.wait_ge(s["stat_rstd"], 1)
            a.activation(col(8), col(14), ACT.Exp, scale=-0.5).then_inc(s["stat_rstd"], 1)

        def halves_pe(pe, s):
            pe.wait_ge(s["stat_mean"], 1)
            pe.matmul(ps[:, 0, 0:2], wa[:, ca["halves"][0]:ca["halves"][1]], col(2, 2),
                      start=True, stop=True).then_inc(s["stat_halves"], 1)

        sa["store_steps"], sbm["store_steps"] = 16, 32

        UB = [0, 1, 2, 0, 1, 2, 0, 1, 2, 3, 0, 1, 2, 3]
        assert len(UB) == ST
        BC = ["bc0", "bc1"]
        AHEAD = [(n, k) for k in range(6) for n in ("lnc", "lnv")] + [(n, 0) for n in ["u", "z", "dt"] + BC] + \
            [(n, 1) for n in ("u", "z", "dt")]
        BASE = len(AHEAD)
        AT = {}
        for t in range(ST):
            for name in TASKS:
                if not name.startswith("ln") or t == 0 or t >= 8:
                    AT[(t, name)] = len(AT)
        TMP = len(AT)
        assert TMP % 2 == 0
        D_BANK, DU_BANK, TMP_BANK, Y_BANK, O_BANK = 0, 2, 4, 6, 7

        class Step:
            def __init__(self, p, t):
                self.p, self.t, self.ahead = p, t, False
                self.tile = p * ST + t
                self.next = p * ST + (t + 1)
                self.next_u = UB[(t + 1) % ST]
                self.par = (t + 1) % 2
                ft = (t + 2) % ST
                self.far = p * ST + (t + 2)
                self.far_s, self.far_k, self.far_u = ft // KT, ft % KT, UB[ft]
                self.far_xn = (p + (t + 2) // ST) * KT + ft % KT + 1
                self.has_ln = t == 0 or t >= 8
                self.ln = p * KT + 6 if t == 0 else p * KT + (KT + t - 8)
                self.ln_k = 6 if t == 0 else t - 8
                self.ln_pair = p if t == 0 else (p + 1) % PAIRS
                self.ln_out = p * ST if t == 0 else p * ST + t

            def tmp(self, name):
                i = AT[(self.t, name)]
                return self.p * TMP + (i + BASE), (i + BASE) % 2

            def two_back(self, name):
                order = [n for n in TASKS if not n.startswith("ln") or self.has_ln]
                i = order.index(name) - 2
                if i < 0:
                    return order[i], self.next - 1 if order[i].startswith("bc") else self.far - 1
                back = order[i]
                return back, self.next if back.startswith("bc") else self.ln if back.startswith("ln") else self.far

        class Ahead:
            def __init__(self, k):
                self.k, self.ahead = k, True
                self.par, self.next, self.next_u = 0, 0, 0
                self.far, self.far_s, self.far_k, self.far_u, self.far_xn = k, 0, k, UB[k], k + 1
                self.ln, self.ln_k, self.ln_pair, self.ln_out = k, k, 0, 0

            def tmp(self, name):
                i = AHEAD.index((name, self.k))
                return i, i % 2

            def two_back(self, name):
                i = AHEAD.index((name, self.k)) - 2
                return AHEAD[i] if i >= 0 else None

        def wait_bank(pe, st, name):
            back = st.two_back(name)
            if back is None:
                return
            back, n = back
            if back.startswith("bc"):
                pe.wait_ge(S["bc_ready"], n * 2 + int(back[2:]) + 1)
            elif back.startswith("ln"):
                pe.wait_ge(S["squared" if back == "lnc" else "var_copied"], n + 1)
            elif back == "z":
                pe.wait_ge(S["sz_ready"], n + 2)
            else:
                pe.wait_ge(S[{"u": "u_ready", "dt": "d_relu"}[back]], n + 1)

        def tmp_pe(pe, st, name, emit):
            n, bank = st.tmp(name)
            wait_bank(pe, st, name)
            emit(ps[:, TMP_BANK + bank, 0:T]).then_inc(S["tmp_done"], 1)

        def conv_tap(pe, st, k):
            n, bank = st.tmp("u")
            if k == 0:
                wait_bank(pe, st, "u")
                pe.wait_ge(S["xn_ready"], st.far_xn)
            a = st.far_k * T + k
            mm = pe.matmul(ps[:, TMP_BANK + bank, 0:T], wtap[:, st.far_s, k, :], xn[:, a:a + T],
                           start=(k == 0), stop=(k == 3))
            if k == 3:
                mm.then_inc(S["tmp_done"], 1)

        def pe_task(pe, st, name):
            if name == "z":
                def emit(o):
                    a = st.far_k * T + 3
                    return pe.matmul(o, wcs("gate_in", st.far_s, P), xn[:, a:a + T], start=True, stop=True)
            elif name == "dt":
                pe.wait_ge(S["u_ready"], st.far + 1)

                def emit(o):
                    return pe.matmul(o, wdt[:, :], u[:, st.far_u, :], start=True, stop=True)
            elif name.startswith("bc"):
                def emit(o):
                    return pe.matmul(o, wcs("spread_bc", int(name[2:]), P), u[:, st.next_u, :], start=True, stop=True)
            elif name == "lnc":
                pe.wait_ge(S["x_relu"], st.ln + 1)

                def emit(o):
                    return pe.matmul(o, wcs("centre", 0, P), xres[:, :], start=True, stop=True)
            else:
                pe.wait_ge(S["squared"], st.ln + 1)

                def emit(o):
                    return pe.matmul(o, wcs("average", 0, P), xsq[:, :], start=True, stop=True)
            tmp_pe(pe, st, name, emit)

        def act_task(a, st, name):
            n, bank = st.tmp(name)
            src = ps[:, TMP_BANK + bank, 0:T]
            a.wait_ge(S["tmp_done"], n + 1)
            if name == "u":
                if not st.ahead:
                    a.wait_ge(S["y_gated"], st.tile + 2)
                a.activation(u[:, st.far_u, :], src, ACT.Silu, bias=vec_c(2)).then_inc(S["u_ready"], 1)
            elif name == "z":
                a.activation(sz[:, st.far_u, :], src, ACT.Silu).then_inc(S["sz_ready"], 1)
            elif name == "dt":
                if not st.ahead or st.k:
                    a.wait_ge(S["delta"], st.far)
                a.activation(dabs[:, :], src, ACT.Abs, bias=vec_c(3)).then_inc(S["d_abs"], 1)
                a.activation(drelu[:, :], src, ACT.Relu, bias=vec_c(3)).then_inc(S["d_relu"], 1)
                a.wait_ge(S["d_abs"], st.far + 1)
                a.activation(dexp[:, :], dabs[:, :], ACT.Exp, scale=-1.0).then_inc(S["d_exp"], 1)
                a.wait_ge(S["d_exp"], st.far + 1)
                a.activation(dln[:, :], dexp[:, :], ACT.Ln, bias=1.0).then_inc(S["d_ln"], 1)
                a.activation(dw[:, :], dexp[:, :], ACT.Identity, bias=1.0).then_inc(S["d_w"], 1)
                a.wait_ge(S["d_w"], st.far + 1)
                a.activation(dq[:, :], dw[:, :], ACT.Identity, bias=vec_c(4)).then_inc(S["d_q"], 1)
            elif name.startswith("bc"):
                if not st.ahead:
                    a.wait_ge(S["prod_done"], st.tile * UN + UN)
                a.copy(bsp[:, st.par, int(name[2:]), :], src).then_inc(S["bc_ready"], 1)
            elif name == "lnc":
                if not (st.ahead and st.k == 0):
                    a.wait_ge(S["scaled"], st.ln)
                a.copy(xcen[:, :], src).then_inc(S["centred"], 1)
                a.activation(xsq[:, :], src, ACT.Square).then_inc(S["squared"], 1)
            else:
                a.activation(xvar[:, :], src, ACT.Ln, bias=vec_c(5)).then_inc(S["var_copied"], 1)
                a.wait_ge(S["var_copied"], st.ln + 1)
                a.activation(xrstd[:, :], xvar[:, :], ACT.Exp, scale=-0.5).then_inc(S["rstd"], 1)

        def ln_load(sp, st):
            if not (st.ahead and st.k == 0):
                sp.wait_ge(S["x_summed"], st.ln)
            a = st.ln_k * T
            for dst, src in ((lnx, x), (lny, y2)):
                v = src.rearrange("(g n) c h w -> g (n c) (h w)", n=2)
                sp.dma_start(dst[:, :], v[st.ln_pair, :, a:a + T]).then_inc(S["ln_loaded"], 16)

        def ln_sum(v, st):
            v.wait_ge(S["ln_loaded"], (st.ln + 1) * 32)
            if not (st.ahead and st.k == 0):
                v.wait_ge(S["x_relu"], st.ln)
            v.scalar_tensor_tensor(xsum[:, :], lny[:, :], col(SCALE2), lnx[:, :], ALU.mult, ALU.add)\
                .then_inc(S["x_summed"], 1)

        def ln_relu(a, st):
            a.wait_ge(S["x_summed"], st.ln + 1)
            if not (st.ahead and st.k == 0):
                a.wait_ge(S["centred"], st.ln)
            a.activation(xres[:, :], xsum[:, :], ACT.Relu, bias=col(SHIFT2)).then_inc(S["x_relu"], 1)

        def ln_scale(v, st):
            v.wait_ge(S["rstd"], st.ln + 1)
            if not (st.ahead and st.k == 0):
                v.wait_ge(S["xn_ready"], st.ln)
            v.scalar_tensor_tensor(xg[:, :], xcen[:, :], vec_c(0), xrstd[:, :], ALU.mult, ALU.mult)\
                .then_inc(S["scaled"], 1)

        def ln_shift(a, st):
            a.wait_ge(S["scaled"], st.ln + 1)
            if not st.ahead:
                a.wait_ge(S["out_mm"], st.ln_out + 2)
            k = st.ln_k * T + 3
            a.activation(xn[:, k:k + T], xg[:, :], ACT.Identity, bias=vec_c(1)).then_inc(S["xn_ready"], 1)

        def delta_log(g, st):
            if not st.ahead:
                g.wait_ge(S["delta"], st.next)
            g.wait_ge(S["d_q"], st.next + 1)
            g.tensor_tensor(ds2[:, :], dexp[:, :], dq[:, :], ALU.subtract).then_inc(S["d_s2"], 1)
            g.wait_ge(S["d_s2"], st.next + 1)
            g.tensor_tensor(ds1[:, :], dln[:, :], ds2[:, :], ALU.add).then_inc(S["d_s1"], 1)

        def delta_min(v, st):
            v.wait_ge(S["d_s1"], st.next + 1)
            v.tensor_tensor(ds1[:, :], ds1[:, :], dexp[:, :], ALU.min).then_inc(S["d_min"], 1)

        def delta_sum(g, st):
            if not st.ahead:
                g.wait_ge(S["split"], st.next)
                g.wait_ge(S["delta_u"], st.next)
            g.wait_ge(S["d_min"], st.next + 1)
            g.tensor_tensor(dlt[:, 0, :], ds1[:, :], drelu[:, :], ALU.add).then_inc(S["delta"], 1)

        def delta_times_u(g, st):
            g.wait_ge(S["delta"], st.next + 1)
            g.wait_ge(S["u_ready"], st.next + 1)
            g.tensor_tensor(dlt[:, 1, :], dlt[:, 0, :], u[:, st.next_u, :], ALU.mult).then_inc(S["delta_u"], 1)

        def cast_part(a, st, part):
            if part == 0:
                a.wait_ge(S["delta_u"], st.next + 1)
                if not st.ahead:
                    a.wait_ge(S["stacked"], st.next * STACKED)
                src = dlt[:, :, :]
            else:
                a.wait_ge(S["rest"], st.next + 1)
                src = rest[:, :, :]
            a.copy(parts[:, :, part, :], src).then_inc(S["cast"], 1)

        def rest_of(v, st, part):
            v.wait_ge(S["cast"], st.next * 2 + part + 1)
            if part == 0:
                v.tensor_tensor(rest[:, :, :], dlt[:, :, :], parts[:, :, 0, :], ALU.subtract).then_inc(S["rest"], 1)
            else:
                v.tensor_tensor(parts[:, :, 2, :], rest[:, :, :], parts[:, :, 1, :], ALU.subtract)\
                    .then_inc(S["split"], 1)

        STACKED = 3 * GR * 16

        def stack_parts(sp, st):
            if not st.ahead:
                sp.wait_ge(S["du_spread"], (st.next - 1) * UN + 1)
                sp.sem_inc(S["gates"], 1)
            for part in range(3):
                if part < 2:
                    sp.wait_ge(S["cast"], st.next * 2 + (part + 1))
                else:
                    sp.wait_ge(S["split"], st.next + 1)
                for grp in range(GR):
                    sp.dma_start(stack[DI * part:DI * (part + 1), st.par, :, grp, :],
                                 parts[DI * grp:DI * (grp + 1), :, part, :]).then_inc(S["stacked"], 16)

        def unit(st, j):
            return (st, j) if j < UN else (Step(st.p, st.t + 1) if st.t + 1 < ST else Step(st.p + 1, 0), j - UN)

        def spread_delta(pe, st, j):
            b, grp = j // GR, j % GR
            if j == 0:
                pe.wait_ge(S["stacked"], (st.tile + 1) * STACKED)
            pe.wait_ge(S["exp_done"], st.tile * UN + j + 1)
            pe.matmul(ps[:, D_BANK + j % 2, 0:T], seld[0:96, b, :], stack[:, st.t % 2, 0, grp, :],
                      start=True, stop=True).then_inc(S["d_spread"], 1)

        def spread_du(pe, st, j):
            b, grp = j // GR, j % GR
            if j == 0:
                pe.wait_ge(S["stacked"], (st.tile + 1) * STACKED)
            pe.wait_ge(S["dbu_done"], st.tile * UN + j + 1)
            pe.matmul(ps[:, DU_BANK + j % 2, 0:T], seld[0:96, b, :], stack[:, st.t % 2, 1, grp, :],
                      start=True, stop=True).then_inc(S["du_spread"], 1)

        def decay(a, st, j):
            n = st.tile * UN + j
            a.wait_ge(S["d_spread"], n + 2)
            a.wait_ge(S["scan_done"], n + 1)
            a.activation(da[:, j % 8, :], ps[:, D_BANK + j % 2, 0:T], ACT.Exp, scale=nega[:, j:j + 1])\
                .then_inc(S["exp_done"], 1)

        def drive(v, st, j):
            n = st.tile * UN + j
            v.wait_ge(S["du_spread"], n + 2)
            if j == 0:
                v.wait_ge(S["bc_ready"], st.tile * 2 + 1)
            v.wait_ge(S["scan_done"], n + 1)
            v.tensor_tensor(dbu[:, j % 8, :], ps[:, DU_BANK + j % 2, 0:T], bsp[:, st.t % 2, 0, :],
                            ALU.mult).then_inc(S["dbu_done"], 1)

        def scan(v, st, j):
            n = st.tile * UN + j
            v.wait_ge(S["exp_done"], n + 3)
            v.wait_ge(S["dbu_done"], n + 3)
            v.wait_ge(S["prod_done"], n + 1)
            first = st.t % KT == 0
            v.tensor_tensor_scan(hs[:, j, :], da[:, j % 8, :], dbu[:, j % 8, :],
                                 0.0 if first else hs[:, j, T - 1:T], ALU.mult, ALU.add)\
                .then_inc(S["scan_done"], 1)

        def times_c(g, st, j):
            n = st.tile * UN + j
            g.wait_ge(S["scan_done"], n + 9)
            if j == 0:
                g.wait_ge(S["bc_ready"], st.tile * 2 + 2)
            if j % GR == 0:
                g.wait_ge(S["y_summed"], st.tile * 4 + j // GR + 3)
            g.tensor_tensor(prod[:, j % 8, :], hs[:, j, :], bsp[:, st.t % 2, 1, :], ALU.mult)\
                .then_inc(S["prod_done"], 1)

        def sum_states(pe, tile, b, ub=None):
            if b == 0:
                pe.wait_ge(S["y_gated"], tile + 2)
                pe.matmul(ps[:, Y_BANK, 0:T], wcs("skip", 0, P), u[:, ub, :], start=True, stop=False)
            for grp in range(GR):
                pe.wait_ge(S["prod_done"], tile * UN + b * GR + grp + 17)
                mm = pe.matmul(ps[DI * grp:DI * (grp + 1), Y_BANK, 0:T], wcs("reduce_n", b, DI),
                               prod[:, (b * GR + grp) % 8, :], start=False, stop=(b == 3))
            mm.then_inc(S["y_summed"], 1)

        def gate(v, tile, ub):
            v.wait_ge(S["y_summed"], tile * 4 + 8)
            v.wait_ge(S["out_mm"], tile + 2)
            v.wait_ge(S["sz_ready"], tile + 2)
            v.tensor_tensor(yg[:, :], ps[:, Y_BANK, 0:T], sz[:, ub, :], ALU.mult).then_inc(S["y_gated"], 1)

        def project_out(pe, tile, s, k):
            pe.wait_ge(S["y_gated"], tile + 3)
            pe.wait_ge(S["out_evac"], tile * 2 + 3)
            for odd, lo in ((1, 0), (0, C)):
                o = ps[lo:lo + C, O_BANK, 0:T // 2]
                pe.matmul(o, wcs("proj_out", 0, C), yg[:, odd:T:2], start=True, stop=False)
                mm = pe.matmul(o, wcs("residual", s, C), xn[:, 3 + k * T + odd:3 + k * T + T:2], start=False, stop=True)
            mm.then_inc(S["out_mm"], 1)

        def evacuate(a, tile, par, n_before):
            a.wait_ge(S["out_mm"], tile + 3)
            a.wait_ge(S[f"out_stored{par}"], n_before * 16 + 16)
            for half, slot in ((0, 1), (1, 0)):
                src = ps[C * half:C * half + C, O_BANK, 0:T // 2].rearrange("p (r j) -> p r j", j=HALF)
                a.copy(otile[C * half:C * half + C, par, :, slot:slot + HALF], src).then_inc(S["out_evac"], 1)

        def store(sp, tile, par, img, k):
            sp.wait_ge(S["out_evac"], tile * 2 + 5)
            sp.dma_start(x3[img, :, k * TR:(k + 1) * TR, :], otile[:, par, :, :]).then_inc(S[f"out_stored{par}"], 16)

        def ended(p, t):
            tile = p * ST + (t - 1)
            tt = (t - 1) % ST
            par = tt % 2
            before = p * KT + (t // 2 if par else (t - 1) // 2)
            img = (p * 2 + (N - 1)) % N if t == 0 else p * 2 + tt // KT
            return tile, UB[tt], tt // KT, tt % KT, par, before, img

        COPIES = 1 + 55 + 28 + 1 + 110

        def steps_of(direction):
            return {0: (1, 55), 1: (56, 110), 2: (112, 166), 3: (167, 221)}[direction]

        def scan_loops(e, body, columns_start=lambda: None):
            for d in range(4):
                lo, hi = steps_of(d)
                m = lo
                if d == 2:
                    columns_start()
                while m % 4:
                    body(d, m, m, m // 2)
                    m += 1
                n = (hi + 1 - m) // 4
                with e.Fori(0, n) as i:
                    for r in range(4):
                        body(d, i * 4 + (m + r), m + r, i * 2 + (m + r) // 2)
                m += 4 * n
                while m <= hi:
                    body(d, m, m, m // 2)
                    m += 1

        def position(d, m):
            return {0: m, 1: 110 - m, 2: m - 111, 3: 221 - m}[d] if isinstance(m, int) else \
                (m if d == 0 else 110 - m if d == 1 else m - 111 if d == 2 else 221 - m)

        def mms_before(d, m):
            return m - 1 if d < 2 else m - 2

        block = ctx.enter_context(nc.Block())

        @block.sync
        def _(sp):
            sp.dma_start(wa[:, :], pack_a).then_inc(pack_in, 16)
            sp.wait_ge(pads_zeroed, 1)

            def load_x(i, b):
                im = i * 2 + b
                rows = x[im].rearrange("c (r two) w -> c r two w", two=2)
                sp.dma_start(xpad[0:C, b, 1:HALF + 1, 1:W + 1], rows[:, :, 1, :]).then_inc(sa[f"in_loaded{b}"], 16)
                sp.dma_start(xpad[C:P, b, 0:HALF, 1:W + 1], rows[:, :, 0, :]).then_inc(sa[f"in_loaded{b}"], 16)

            load_x(0, 0)
            load_x(0, 1)
            with sp.Fori(0, PAIRS - 1) as i:
                for b in range(2):
                    sp.wait_ge(sa["split"], i * 2 + (b + 1))
                    load_x(i + 1, b)
            barrier(sp, 1)
            sp.dma_start(yin[:, 0, :], y1[0]).then_inc(sbm["in_loaded0"], 16)
            sp.dma_start(yin[:, 1, :], y1[1]).then_inc(sbm["in_loaded1"], 16)
            with sp.Fori(0, PAIRS - 1) as i:
                for b in range(2):
                    sp.wait_ge(sbm["padded"], i * 4 + (b + 1) * 2)
                    sp.dma_start(yin[:, b, :], y1[i * 2 + (2 + b)]).then_inc(sbm[f"in_loaded{b}"], 16)
            barrier(sp, 2)
            sp.dma_start(wc[:, :], pack_c).then_inc(pack_in, 16)
            for k in range(6):
                ln_load(sp, Ahead(k))
            st = Ahead(0)
            stack_parts(sp, st)
            with sp.Fori(0, PAIRS) as p:
                for t in range(ST):
                    st = Step(p, t)
                    tile, ub, s, k, par, before, img = ended(p, t)
                    if st.has_ln:
                        ln_load(sp, st)
                    stack_parts(sp, st)
                    store(sp, tile, par, img, k)
            tile, ub, s, k, par, before, img = ended(PAIRS, 0)
            store(sp, tile, par, N - 1, k)
            sp.wait_ge(S["out_stored1"], (before + 2) * 16)
            sp.wait_ge(S["out_stored0"], (before + 1) * 16)
            barrier(sp, 3)
            sp.dma_start(wd[:, :], pack_d).then_inc(pack_in, 16)
            sp.dma_start(ws[:, :], pack_s).then_inc(pack_in, 16)
            sp.wait_ge(D["zeroed"], 1)
            with sp.Fori(0, N // 2) as i:
                for b in range(2):
                    sp.wait_ge(D["conv_done"], i * 8 + b * QT + 4)
                    sp.dma_start(xpad3[:, b, 1:H + 1, :], x3[i * 2 + b]).then_inc(D[f"loaded{b}"], 16)

        @block.tensor
        def _(pe):
            conv_pe(pe, sa, 0)
            halves_pe(pe, sa)
            barrier(pe, 1)
            conv_pe(pe, sbm, 1)
            halves_pe(pe, sbm)
            barrier(pe, 2)
            pe.wait_ge(pack_in, 32)
            pe.matmul(ps[:, 0, 0:P], wcs("dt_rows", 0, P)[0:HC, :], wcs("dt_rows", 1, P)[0:HC, :],
                      start=True, stop=True).then_inc(S["wdt_mm"], 1)
            pe.wait_ge(S["ready"], 4)
            for k in range(6):
                st = Ahead(k)
                pe_task(pe, st, "lnc")
                pe_task(pe, st, "lnv")
            st = Ahead(0)
            for k in range(4):
                conv_tap(pe, st, k)
            for name in ["z", "dt"] + BC:
                pe_task(pe, st, name)
            st = Ahead(1)
            for k in range(4):
                conv_tap(pe, st, k)
            pe_task(pe, st, "z")
            pe_task(pe, st, "dt")
            for b in range(3):
                sum_states(pe, -1, b, UB[-1])
            for j in range(max(LEAD["delta"], LEAD["du"])):
                if j < LEAD["du"]:
                    spread_du(pe, Step(0, 0), j)
                if j < LEAD["delta"]:
                    spread_delta(pe, Step(0, 0), j)
            with pe.Fori(0, PAIRS) as p:
                for t in range(ST):
                    st = Step(p, t)
                    tile, ub, s, k, par, before, img = ended(p, t)
                    for j in range(UN):
                        spread_du(pe, *unit(st, j + LEAD["du"]))
                        spread_delta(pe, *unit(st, j + LEAD["delta"]))
                        for name in PE_AT.get(j, ()):
                            if name == "project":
                                project_out(pe, tile, s, k)
                            elif name == "last3":
                                sum_states(pe, tile, 3)
                            elif name.startswith("sum"):
                                sum_states(pe, st.tile, int(name[3:]), UB[t])
                            elif name.startswith("tap"):
                                conv_tap(pe, st, int(name[3:]))
                            elif st.has_ln or not name.startswith("ln"):
                                pe_task(pe, st, name)
            tile, ub, s, k, par, before, img = ended(PAIRS, 0)
            sum_states(pe, tile, 3)
            project_out(pe, tile, s, k)
            barrier(pe, 3)
            pe.wait_ge(pack_in, 64)
            a = cd["w2"][0]
            for tap in range(9):
                mm = pe.matmul(ps[:, tap // 5, (tap % 5) * (C + 1):(tap % 5 + 1) * (C + 1)],
                               wd[:, a + tap * P:a + (tap + 1) * P], wd[:, cd["w1b1"][0]:cd["w1b1"][1]],
                               start=True, stop=True)
            mm.then_inc(D["prep_mm"], 1)
            pe.wait_ge(D["prep_v"], 2)
            w3 = wd[:, cd["w3"][0]:cd["w3"][1]]
            for tap in range(9):
                for half in range(2):
                    pe.matmul(ps[C * half:C * half + C, 2 + tap // 5, (tap % 5) * C:(tap % 5 + 1) * C],
                              rmix[:, tap, 0:C], w3, start=True, stop=True)
            for half in range(2):
                o = slice(C * half, C * half + C)
                pe.matmul(ps[o, 4, 0:9], w3, rmix[:, :, C:C + 1].rearrange("p a b -> p (a b)"), start=True, stop=True)
                pe.matmul(ps[o, 5, 0:1], w3, wd[:, cd["b2"][0]:cd["b2"][1]], start=True, stop=False)
                mm = pe.matmul(ps[o, 5, 0:1], wd[:, cd["b3"][0]:cd["b3"][1]], wd[:, cd["ones"][0]:cd["ones"][1]],
                               start=False, stop=True)
            mm.then_inc(D["prep_mm"], 1)
            pe.wait_ge(D["bias_ready"], 1)
            with pe.Fori(0, 2) as g:
                for ch in range(2):
                    pe.wait_ge(D[f"row{ch}"], g * 220 + 1)
                pe.sem_inc(D["gates"], 1)
                with pe.Fori(0, GRP // 2) as i:
                    for b in range(2):
                        pe.wait_ge(D[f"loaded{b}"], (g * (GRP // 2) + i) * 16 + 16)
                        for q in range(QT):
                            pe.wait_ge(D["evacuated"], (g * (GRP // 2) + i) * 8 + b * QT + q + 1)
                            for ky in range(3):
                                for ab in range(2):
                                    mm = pe.matmul(ps[:, b * QT + q, 0:QN], lw[:, ky * 2 + ab, :],
                                                   xpad3[:, b, q * (H // QT) + ky:(q + 1) * (H // QT) + ky, ab:ab + HALF],
                                                   start=(ky + ab == 0), stop=(ky + ab == 3))
                            mm.then_inc(D["conv_done"], 1)

                def body(d, m, mi, half):
                    for ch in range(2):
                        if mi == 1:
                            pe.wait_ge(D[f"copied{ch}"], g * COPIES + 1)
                        else:
                            pe.wait_ge(D[f"row{ch}"], g * 220 + mms_before(d, m) + 1)
                        for s in range(KS):
                            w0 = (d * KS + s) * P
                            mm = pe.matmul(ps[:, 2 * ch + mi % 2, 0:CH * HALF], ws[:, w0:w0 + P],
                                           pv[:, ch, (mi - 1) % 4, :, s:s + HALF], start=(s == 0), stop=(s == KS - 1))
                        mm.then_inc(D[f"mm{ch}"], 1)

                def columns_start():
                    for ch in range(2):
                        pe.wait_ge(D[f"copied{ch}"], g * COPIES + 85)
                    pe.sem_inc(D["gates"], 1)
                scan_loops(pe, body, columns_start)

        @block.scalar
        def _(a):
            a.wait_ge(pack_in, 16)
            a.activation(signs[:, 0, :, :], wa[:, ca["conv1"][0]:ca["conv1"][1]].rearrange("p (t m) -> p t m", m=P),
                         ACT.Sign).then_inc(sa["weights_ready"], 1)
            a.activation(signs[:, 1, :, :], wa[:, ca["conv2"][0]:ca["conv2"][1]].rearrange("p (t m) -> p t m", m=P),
                         ACT.Sign).then_inc(sbm["weights_ready"], 1)
            def store_y1(i, b):
                a.wait_ge(sa["out_ready"], i * 8 + (b + 1) * QT)
                a.dma_start(y1[i * 2 + b], yout[:, b, :]).then_inc(sa[f"stored{b}"], 16)

            with a.Fori(0, PAIRS) as i:
                for b in range(2):
                    store_y1(i, b)
            for b in range(2):
                a.wait_ge(sa[f"stored{b}"], 16 * PAIRS + 16)
            rstd_act(a, sa)
            barrier(a, 1)
            def norm(i, b, first):
                a.wait_ge(sbm[f"in_loaded{b}"], (i + 1) * 16)
                if not first:
                    a.wait_ge(sbm["split"], i * 2 + (b - 1))
                for half, slot in ((0, 1), (1, 0)):
                    o = slice(C * half, C * half + C)
                    a.activation(xpad[o, b, slot:slot + HALF, 1:W + 1],
                                 yin[o, b, :].rearrange("p (r w) -> p r w", w=W), ACT.Relu,
                                 bias=bn[o, SHIFT1:SHIFT1 + 1], scale=bn[o, SCALE1:SCALE1 + 1]).then_inc(sbm["padded"], 1)

            def put(i, b):
                a.wait_ge(sbm["out_ready"], i * 8 + (b + 1) * QT)
                rows = y2[i * 2 + b].rearrange("c (r two) w -> c r two w", two=2)
                for half, odd in ((0, 1), (1, 0)):
                    a.dma_start(rows[:, :, odd, :], yout[C * half:C * half + C, b, :].rearrange("p (r w) -> p r w", w=W))\
                        .then_inc(sbm[f"stored{b}"], 16)
            norm(0, 0, True)
            norm(0, 1, True)
            with a.Fori(0, PAIRS - 1) as i:
                for b in range(2):
                    norm(i + 1, b, False)
                    put(i, b)
            put(PAIRS - 1, 0)
            put(PAIRS - 1, 1)
            for b in range(2):
                a.wait_ge(sbm[f"stored{b}"], 32 * PAIRS + 16)
            rstd_act(a, sbm)
            barrier(a, 2)
            a.wait_ge(pack_in, 32)
            a.preload_act_table_set("natural_log_exp_and_others")
            a.activation(nega[:, :], wcs("a_log", 0, UN), ACT.Exp).then_inc(S["prep"], 1)
            a.wait_ge(S["prep"], 1)
            a.activation(nega[:, :], nega[:, :], ACT.Copy, scale=-1.0).then_inc(S["ready"], 1)
            a.wait_ge(S["ready"], 4)
            for k in range(6):
                st = Ahead(k)
                ln_relu(a, st)
                act_task(a, st, "lnc")
                act_task(a, st, "lnv")
                ln_shift(a, st)
            for k in range(2):
                st = Ahead(k)
                a.preload_act_table_set("silu_and_others")
                act_task(a, st, "u")
                act_task(a, st, "z")
                a.preload_act_table_set("natural_log_exp_and_others")
                act_task(a, st, "dt")
                if k == 0:
                    for name in BC:
                        act_task(a, st, name)
                    for part in range(2):
                        cast_part(a, st, part)
            for j in range(LEAD["decay"]):
                decay(a, Step(0, 0), j)
            with a.Fori(0, PAIRS) as p:
                for t in range(ST):
                    st = Step(p, t)
                    tile, ub, s, k, par, before, img = ended(p, t)
                    for j in range(UN):
                        decay(a, *unit(st, j + LEAD["decay"]))
                        for name in ACT_AT.get(j, ()):
                            if name == "silu":
                                a.preload_act_table_set("silu_and_others")
                            elif name == "exp":
                                a.preload_act_table_set("natural_log_exp_and_others")
                            elif name.startswith("cast"):
                                cast_part(a, st, int(name[4]))
                            elif name == "evacuate":
                                evacuate(a, tile, par, before)
                            elif name == "relu":
                                if st.has_ln:
                                    ln_relu(a, st)
                            elif name == "shift":
                                if st.has_ln:
                                    ln_shift(a, st)
                            elif st.has_ln or not name.startswith("ln"):
                                act_task(a, st, name)
            tile, ub, s, k, par, before, img = ended(PAIRS, 0)
            evacuate(a, tile, par, before)
            barrier(a, 3)
            with a.Fori(0, 2) as g:
                for ch in range(2):
                    a.wait_ge(D["evacuated"], (g + 1) * GRP * QT + 8)
                    a.copy(pv[:, ch, 0, :, PADS:PADS + HALF], R[:, ch * CH:(ch + 1) * CH, 0:HALF])\
                        .then_inc(D[f"copied{ch}"], 1)

                def body(d, m, mi, half):
                    r = position(d, m)
                    for ch in range(2):
                        im = slice(ch * CH, (ch + 1) * CH)
                        new = pv[:, ch, mi % 4, :, PADS:PADS + HALF]
                        if d == 0:
                            a.wait_ge(D[f"row{ch}"], g * 220 + m + 1)
                            a.copy(R[:, im, bass.ds(r * HALF, HALF)], new).then_inc(D[f"copied{ch}"], 1)
                        elif d == 1:
                            if mi % 2:
                                continue
                            a.wait_ge(D[f"row{ch}"], g * 220 + m + 1)
                            a.wait_ge(D[f"copied{ch}"], g * COPIES + 28 + half)
                            for odd in range(2):
                                for wp in range(2):
                                    o = slice(0, C) if odd else slice(C, P)
                                    i_ = slice(0, C) if wp else slice(C, P)
                                    dst = R[o, im, bass.ds(r * HALF, 2 * HALF)].rearrange("p n (j two) -> p n j two", two=2)
                                    ins = a.copy(dst[:, :, :, wp],
                                                 pv[i_, ch, (mi - odd) % 4, :, PADS:PADS + HALF])
                            ins.then_inc(D[f"copied{ch}"], 1)
                        else:
                            a.wait_ge(D[f"row{ch}"], g * 220 + mms_before(d, m) + 2)
                            a.wait_ge(D[f"copied{ch}"], g * COPIES + (m - 28 if d == 3 else 85))
                            dst = R[:, im, :].rearrange("p n (j w) -> p n j w", w=W)
                            a.copy(dst[:, :, :, bass.ds(r, 1)].rearrange("p n j w -> p n (j w)"), new)\
                                .then_inc(D[f"copied{ch}"], 1)
                        if mi == 110:
                            a.wait_ge(D[f"copied{ch}"], g * COPIES + 56 + 28)
                            src = R[:, im, :].rearrange("p n (j w) -> p n j w", w=W)
                            a.copy(pv[:, ch, 3, :, PADS:PADS + HALF], src[:, :, :, 0]).then_inc(D[f"copied{ch}"], 1)
                scan_loops(a, body)
                for ch in range(2):
                    a.wait_ge(D[f"copied{ch}"], (g + 1) * COPIES)
                    a.sem_inc(D["gates"], 1)
                    with a.Fori(0, CH) as n:
                        for half in range(2):
                            rows = out[g * GRP + n + ch * CH].rearrange("c (r two) w -> c r two w", two=2)
                            a.dma_start(rows[:, :, 1 - half, :],
                                        R[C * half:C * half + C, n + ch * CH, :].rearrange("p (r w) -> p r w", w=W))\
                                .then_inc(D[f"stored{ch}"], 16)
            for ch in range(2):
                a.wait_ge(D[f"stored{ch}"], 2 * CH * 32 + 16)

        @block.vector
        def _(v):
            v.memset(xpad[:, :, :, :], 0.0).then_inc(pads_zeroed, 1)
            v.sem_inc(sa["psum_free"], 8)
            v.sem_inc(sbm["psum_free"], 8)
            for b in range(2):
                v.sem_inc(sa[f"stored{b}"], 16)
                v.sem_inc(sbm[f"stored{b}"], 16)
            v.sem_inc(sa["conv_done"], 4)
            v.sem_inc(sbm["conv_done"], 4)
            convs_dve(v, sa, lambda i, b: (sa[f"in_loaded{b}"], i * 32 + 32))
            batch_stats(v, sa, 0, SCALE1, SHIFT1)
            barrier(v, 1)
            convs_dve(v, sbm, lambda i, b: (sbm["padded"], i * 4 + (b + 1) * 2))
            batch_stats(v, sbm, 2, SCALE2, SHIFT2)
            barrier(v, 2)
            v.memset(xn[:, :], 0.0)
            v.memset(u[:, 3, :], 0.0)
            v.memset(otile[:, :, :, :], 0.0)
            v.memset(hs[:, :, :], 0.0).then_inc(S["ready"], 1)
            v.wait_ge(pack_in, 32)
            for s in range(2):
                for k in range(4):
                    ins = v.tensor_tensor(wtap[:, s, k, :], wcs("conv_in", s, P), wcs("taps", k, P), ALU.mult)
            v.tensor_copy(seld[:, :, :], wc[:, cc["select_d"][0]:cc["select_d"][1]].rearrange("p (b m) -> p b m", m=P))
            v.wait_ge(S["wdt_mm"], 1)
            v.tensor_copy(wdt[:, :], ps[:, 0, 0:P]).then_inc(S["ready"], 1)
            v.wait_ge(S["ready"], 4)
            v.sem_inc(S["exp_done"], 2)
            v.sem_inc(S["dbu_done"], 2)
            v.sem_inc(S["scan_done"], 8)
            v.sem_inc(S["prod_done"], 16)
            for name in ("d_spread", "du_spread", "y_gated", "out_mm", "sz_ready", "out_evac"):
                v.sem_inc(S[name], 1)
            for par in range(2):
                v.sem_inc(S[f"out_stored{par}"], 16)
            for k in range(6):
                st = Ahead(k)
                ln_sum(v, st)
                ln_scale(v, st)
            st = Ahead(0)
            delta_min(v, st)
            for part in range(2):
                rest_of(v, st, part)
            for j in range(LEAD["drive"]):
                drive(v, Step(0, 0), j)
            with v.Fori(0, PAIRS) as p:
                for t in range(ST):
                    st = Step(p, t)
                    tile, ub, s, k, par, before, img = ended(p, t)
                    for j in range(UN):
                        drive(v, *unit(st, j + LEAD["drive"]))
                        scan(v, st, j)
                        for name in DVE_AT.get(j, ()):
                            if name == "min":
                                delta_min(v, st)
                            elif name.startswith("rest"):
                                rest_of(v, st, int(name[4]))
                            elif name == "gate":
                                gate(v, tile, ub)
                            elif name == "add_x":
                                if st.has_ln:
                                    ln_sum(v, st)
                            elif st.has_ln:
                                ln_scale(v, st)
            tile, ub, s, k, par, before, img = ended(PAIRS, 0)
            gate(v, tile, ub)
            barrier(v, 3)
            v.memset(xpad3[:, :, :, :], 0.0).then_inc(D["zeroed"], 1)
            v.sem_inc(D["conv_done"], 8)
            v.sem_inc(D["stored0"], 16)
            v.sem_inc(D["stored1"], 16)
            v.sem_inc(D["row0"], 1)
            v.sem_inc(D["row1"], 1)
            v.memset(pv[:, :, :, :, :], 0.0)
            v.memset(lw[:, :, :], 0.0)
            v.wait_ge(D["prep_mm"], 1)
            n = [0]

            def step(ins):
                n[0] += 1
                ins.then_inc(D["prep_v"], 1)
                v.wait_ge(D["prep_v"], n[0])
            step(v.tensor_copy(rmix[:, 0:5, :], ps[:, 0, 0:5 * (C + 1)].rearrange("p (t c) -> p t c", c=C + 1)))
            step(v.tensor_copy(rmix[:, 5:9, :], ps[:, 1, 0:4 * (C + 1)].rearrange("p (t c) -> p t c", c=C + 1)))
            v.wait_ge(D["prep_mm"], 2)
            lo, hi = slice(0, C), slice(C, P)

            def tap(part, ky, kx):
                i = ky * 3 + kx
                return ps[part, 2 + i // 5, (i % 5) * C:(i % 5 + 1) * C]
            ident = wd[:, cd["ident"][0]:cd["ident"][1]]
            for ky in range(3):
                for ab, kin, kout, kx in ((0, lo, hi, 0), (0, hi, lo, 0), (0, hi, hi, 1),
                                          (1, lo, lo, 1), (1, lo, hi, 2), (1, hi, lo, 2)):
                    dst = lw[kin, ky * 2 + ab, kout]
                    if (ky, kx) == (1, 1):
                        ins = v.tensor_tensor(dst, tap(kin, ky, kx), ident[kin, :], ALU.add)
                    else:
                        ins = v.tensor_copy(dst, tap(kin, ky, kx))
            step(ins)
            step(v.tensor_copy(bt[:, 0:9], ps[:, 4, 0:9]))
            step(v.tensor_copy(bt[:, 9:10], ps[:, 5, 0:1]))
            step(v.tensor_reduce(bt[:, 10:11], bt[:, 0:10], mybir.AxisListType.X, ALU.add))
            step(v.memset(bmap[:, :, :], 0.0))
            step(v.tensor_scalar(bmap[:, :, :], bmap[:, :, :], bt[:, 10:11], None, ALU.add))

            def drop(part, rows, cols, taps, op):
                for i in taps:
                    ap = bmap[part, rows, cols]
                    step(v.tensor_scalar(ap, ap, bt[part, i:i + 1], None, op))
            every = slice(0, P)
            drop(every, slice(0, 1), slice(0, HALF), (0, 1, 2), ALU.subtract)
            drop(every, slice(H - 1, H), slice(0, HALF), (6, 7, 8), ALU.subtract)
            drop(hi, slice(0, H), slice(0, 1), (0, 3, 6), ALU.subtract)
            drop(lo, slice(0, H), slice(HALF - 1, HALF), (2, 5, 8), ALU.subtract)
            for part, cl, r, i in ((hi, 0, 0, 0), (lo, HALF - 1, 0, 2), (hi, 0, H - 1, 6), (lo, HALF - 1, H - 1, 8)):
                drop(part, slice(r, r + 1), slice(cl, cl + 1), (i,), ALU.add)
            v.sem_inc(D["evacuated"], 8)
            v.sem_inc(D["bias_ready"], 1)
            bm = bmap[:, :, :].rearrange("p h j -> p (h j)")
            with v.Fori(0, 2) as g:
                for ch in range(2):
                    v.wait_ge(D[f"stored{ch}"], g * CH * 32 + 16)
                    v.sem_inc(D["gates"], 1)
                    with v.Fori(0, CH // 2) as i:
                        for b in range(2):
                            for q in range(QT):
                                done = (g * (GRP // 2) + i) * 8 + (ch * CH + b) * QT + q + 1
                                v.wait_ge(D["conv_done"], done + 8)
                                v.tensor_tensor(R[:, i * 2 + (ch * CH + b), q * QN:(q + 1) * QN],
                                                ps[:, b * QT + q, 0:QN], bm[:, q * QN:(q + 1) * QN], ALU.add)\
                                    .then_inc(D["evacuated"], 1)
                v.wait_ge(D["evacuated"], (g + 1) * GRP * QT + 8)

                def copied_by(d, m, mi, half):
                    if d == 0:
                        return m - 3
                    if d == 1:
                        return half + 27 + mi % 2
                    if mi == 167:
                        return 139
                    return m - 30

                def body(d, m, mi, half):
                    r = position(d, m)
                    for ch in range(2):
                        im = slice(ch * CH, (ch + 1) * CH)
                        v.wait_ge(D[f"mm{ch}"], g * 220 + mms_before(d, m) + 1)
                        if mi >= 4:
                            v.wait_ge(D[f"copied{ch}"], g * COPIES + copied_by(d, m, mi, half))
                        if d < 2:
                            cur = R[:, im, bass.ds(r * HALF, HALF)]
                        else:
                            cur = R[:, im, :].rearrange("p n (j w) -> p n j w", w=W)[:, :, :, bass.ds(r, 1)]\
                                .rearrange("p n j w -> p n (j w)")
                        v.scalar_tensor_tensor(pv[:, ch, mi % 4, :, PADS:PADS + HALF],
                                               ps[:, 2 * ch + mi % 2, 0:CH * HALF].rearrange("p (n j) -> p n j", j=HALF),
                                               0.0, cur, ALU.max, ALU.add).then_inc(D[f"row{ch}"], 1)

                def columns_start():
                    for ch in range(2):
                        v.wait_ge(D[f"copied{ch}"], g * COPIES + 85)
                    v.sem_inc(D["gates"], 1)
                scan_loops(v, body, columns_start)

        @block.gpsimd
        def _(g):
            barrier(g, 1)
            barrier(g, 2)
            g.memset(prod[:, :, :], 0.0)
            g.memset(sz[:, 3, :], 0.0).then_inc(S["ready"], 1)
            g.wait_ge(S["ready"], 4)
            st = Ahead(0)
            delta_log(g, st)
            delta_sum(g, st)
            delta_times_u(g, st)
            with g.Fori(0, PAIRS) as p:
                for t in range(ST):
                    st = Step(p, t)
                    for j in range(UN):
                        times_c(g, st, j)
                        for name in POOL_AT.get(j, ()):
                            if name == "delta_log":
                                delta_log(g, st)
                            elif name == "delta":
                                delta_sum(g, st)
                            else:
                                delta_times_u(g, st)
            barrier(g, 3)


def pack(np, parts, layout):
    cols, n = columns(layout)
    out = np.zeros((P, n), np.float32)
    for name, a in parts.items():
        lo, hi = cols[name]
        out[:a.shape[0], lo:hi] = a.reshape(a.shape[0], hi - lo)
    return out


def pair_blocks(np, w):
    o = np.zeros((2, C, 3, 2, 2, C), np.float32)
    for ab, kin, kout, ky in ((0, 0, 1, 0), (0, 1, 0, 0), (0, 1, 1, 1), (1, 0, 0, 1), (1, 0, 1, 2), (1, 1, 0, 2)):
        for kx in range(3):
            o[kin, :, kx, ab, kout, :] = w[ky, kx]
    return o.reshape(P, 6 * P)


def scan_blocks(np, k):
    o = np.zeros((2, C, KS, 2, C), np.float32)
    for s in range(KS):
        for kin in range(2):
            for kout in range(2):
                tap = 2 * (s - 2) + (1 - kin) - (1 - kout) + 4
                if 0 <= tap < KW:
                    o[kin, :, s, kout, :] = k[tap]
    return o.reshape(P, KS * P)


def lay_out(np, a):
    eye = np.eye(C, dtype=np.float32)
    two = lambda v: np.concatenate([v, v])[:, None]
    c1, c2 = a["L0_conv_w1"].transpose(2, 3, 1, 0), a["L0_conv_w2"].transpose(2, 3, 1, 0)
    pa = pack(np, {
        "conv1": pair_blocks(np, c1), "conv2": pair_blocks(np, c2),
        "halves": np.tile(eye / 2, (2, 2)),
        "vecs": np.concatenate([two(a[f"L0_conv_{n}"]) for n in ("gamma1", "beta1", "gamma2", "beta2")]
                               + [np.full((P, 1), EPS, np.float32)], 1)}, PACK_A)
    ip = a["L1_conv_in_proj_w"]
    cm = C // HC
    n8 = DI // GR
    by_group = lambda v: v.reshape((GR, n8) + v.shape[1:])
    conv_in, gate_in = (np.zeros((2, HC, cm, 2, GR, HC, n8), np.float32) for _ in range(2))
    out_w = np.zeros((GR, HC, n8, HC, cm), np.float32)
    bc = np.zeros((GR, HC, n8, 2, HC, 2, NS), np.float32)
    dtr = np.zeros((HC, 2, GR, HC, n8), np.float32)
    xp = a["L1_conv_x_proj_w"]
    for c in range(HC):
        for s in range(2):
            conv_in[s, c, :, s, :, c, :] = by_group(ip[:DI]).transpose(2, 0, 1)
            gate_in[s, c, :, s, :, c, :] = by_group(ip[DI:]).transpose(2, 0, 1)
        out_w[:, c, :, c, :] = by_group(np.ascontiguousarray(a["L1_conv_out_proj_w"].T))
        for i in range(2):
            bc[:, c, :, i, c] = by_group(np.ascontiguousarray(xp[1 + NS * i:1 + NS * (i + 1)].T))[:, :, None, :]
        dtr[c, 0, :, c] = by_group(xp[0])
        dtr[c, 1, :, c] = by_group(a["L1_conv_dt_proj_w"][:, 0])
    place = lambda v: np.broadcast_to(by_group(v)[:, None], (GR, HC, n8) + v.shape[1:]).reshape((P,) + v.shape[1:])
    four = lambda v: place(v)[:, None]
    sel_d = np.zeros((3, HC, n8, 4, HC, 2, NS), np.float32)
    red = np.zeros((HC, 2, NS, 4, HC, n8), np.float32)
    for b in range(4):
        for c in range(HC):
            for k in range(2):
                sel_d[:, c, 2 * b + k, b, c, k, :] = 1
                red[c, k, :, b, c, 2 * b + k] = 1
    al = a["L1_conv_A_log"].reshape(GR, 4, 2, NS).transpose(2, 3, 1, 0).reshape(2 * NS, 16)
    block = np.zeros((2, C, 2, C), np.float32)
    for s in range(2):
        block[s, :, s] = 1 / C
    mean = block.reshape(P, P)
    res = np.zeros((2, C, 2, C), np.float32)
    for s in range(2):
        res[s, :, s] = eye
    pc = pack(np, {
        "conv_in": conv_in.reshape(P, 2 * P), "gate_in": gate_in.reshape(P, 2 * P),
        "taps": np.broadcast_to(place(a["L1_conv_conv_w"]).T.reshape(1, 4 * P), (P, 4 * P)),
        "skip": np.diag(place(a["L1_conv_D"])), "spread_bc": bc.reshape(P, 2 * P),
        "select_d": sel_d.reshape(96, 4 * P), "reduce_n": red.reshape(P, 4 * DI),
        "proj_out": out_w.reshape(P, C), "residual": res.reshape(P, 2 * C),
        "centre": np.eye(P, dtype=np.float32) - mean, "average": mean, "dt_rows": dtr.reshape(HC, 2 * P),
        "vecs": np.concatenate([two(a["L1_conv_ln_g"]), two(a["L1_conv_ln_b"]), four(a["L1_conv_conv_b"]),
                                four(a["L1_conv_dt_proj_b"]), np.full((P, 1), -1, np.float32),
                                np.full((P, 1), EPS, np.float32)], 1),
        "a_log": np.tile(al, (HC, 1))}, PACK_C)
    w2 = np.zeros((32, 4, 9, 32, 4), np.float32)
    for g in range(32):
        w2[g, :, :, g, :] = a["L2_conv_W2"][g].transpose(1, 2, 3, 0).reshape(4, 9, 4)
    pd = pack(np, {
        "w1b1": np.concatenate([a["L2_conv_W1"].reshape(P, C), a["L2_conv_b1"].reshape(P, 1)], 1),
        "w2": w2.reshape(P, 9 * P), "w3": a["L2_conv_W3"].transpose(0, 2, 1).reshape(P, C),
        "ident": np.tile(eye, (2, 1)), "b3": a["L2_conv_b3"], "ones": np.ones((P, 1), np.float32),
        "b2": a["L2_conv_b2"].reshape(P, 1)}, PACK_D)
    psc = pack(np, {"scan": np.concatenate([scan_blocks(np, a[f"L3_conv_k_{n}"]) for n in ("td", "dt", "lr", "rl")], 1)},
               PACK_S)
    return {"x": np.ascontiguousarray(a["x"]), "pack_a": pa, "pack_c": pc, "pack_d": pd, "pack_s": psc}


def kernel(**inputs):
    import numpy as _np
    import concourse.bacc as _bacc
    from concourse import mybir as _mybir
    from concourse.bass_utils import run_bass_kernel_spmd as _run

    nc = _bacc.Bacc("TRN2", target_bir_lowering=False, num_devices=1)
    arrays = lay_out(_np, {k: _np.asarray(v) for k, v in inputs.items()})
    aps = [nc.dram_tensor(f"in_{n}", v.shape, _mybir.dt.float32, kind="ExternalInput").ap() for n, v in arrays.items()]
    out = nc.dram_tensor("out_0", arrays["x"].shape, _mybir.dt.float32, kind="ExternalOutput").ap()
    build(nc, *aps, out)
    r = _run(nc, [{f"in_{n}": v for n, v in arrays.items()}], core_ids=[0])
    return r.results[0]["out_0"]
```
